# Optimizing a Trainium2 kernel written in Bass

```python
import numpy as np
import jax
import jax.numpy as jnp

def _softmax(x, axis=-1):
    return jax.nn.softmax(x, axis=axis)

def _gelu(x):
    return jax.nn.gelu(x, approximate=True)

def _silu(x):
    return jax.nn.silu(x)

def _sigmoid(x):
    return jax.nn.sigmoid(x)

def _layernorm(x, axis=-1, eps=1e-05):
    m = jnp.mean(x, axis=axis, keepdims=True)
    v = jnp.var(x, axis=axis, keepdims=True)
    return (x - m) / jnp.sqrt(v + eps)

def _scatter_add(tgt, idx, src, axis=0):
    return tgt.at[idx].add(src)

def _segment_sum(src, seg, n):
    return jax.ops.segment_sum(src, seg, n)
kernel_name = 'mk_dlrm_tower_d1_rec_r8_5a60a1'

def setup_inputs(seed: int=0):
    np.random.seed(seed)
    _w = jnp.asarray

    def _rec_inputs():
        import jax
        import jax.numpy as jnp
        _tk = jax.random.key(seed)
        ids = jnp.stack([jax.random.randint(jax.random.fold_in(_tk, 200 + f), (512,), 0, v, jnp.int32) for f, v in enumerate([1250, 12500, 1000, 1000, 1250, 1250, 1000, 1000, 1000, 12500, 125000, 12500, 1250, 12500, 12500, 12500, 1250, 12500, 12500, 1000, 1250, 1000, 1250, 1000, 1250, 1000])], axis=1)
        tbl_0 = 0.05 * jax.random.normal(jax.random.fold_in(_tk, 500 + 0), (1250, 128), jnp.float32)
        tbl_1 = 0.05 * jax.random.normal(jax.random.fold_in(_tk, 500 + 1), (12500, 128), jnp.float32)
        tbl_2 = 0.05 * jax.random.normal(jax.random.fold_in(_tk, 500 + 2), (1000, 128), jnp.float32)
        tbl_3 = 0.05 * jax.random.normal(jax.random.fold_in(_tk, 500 + 3), (1000, 128), jnp.float32)
        tbl_4 = 0.05 * jax.random.normal(jax.random.fold_in(_tk, 500 + 4), (1250, 128), jnp.float32)
        tbl_5 = 0.05 * jax.random.normal(jax.random.fold_in(_tk, 500 + 5), (1250, 128), jnp.float32)
        tbl_6 = 0.05 * jax.random.normal(jax.random.fold_in(_tk, 500 + 6), (1000, 128), jnp.float32)
        tbl_7 = 0.05 * jax.random.normal(jax.random.fold_in(_tk, 500 + 7), (1000, 128), jnp.float32)
        tbl_8 = 0.05 * jax.random.normal(jax.random.fold_in(_tk, 500 + 8), (1000, 128), jnp.float32)
        tbl_9 = 0.05 * jax.random.normal(jax.random.fold_in(_tk, 500 + 9), (12500, 128), jnp.float32)
        tbl_10 = 0.05 * jax.random.normal(jax.random.fold_in(_tk, 500 + 10), (125000, 128), jnp.float32)
        tbl_11 = 0.05 * jax.random.normal(jax.random.fold_in(_tk, 500 + 11), (12500, 128), jnp.float32)
        tbl_12 = 0.05 * jax.random.normal(jax.random.fold_in(_tk, 500 + 12), (1250, 128), jnp.float32)
        tbl_13 = 0.05 * jax.random.normal(jax.random.fold_in(_tk, 500 + 13), (12500, 128), jnp.float32)
        tbl_14 = 0.05 * jax.random.normal(jax.random.fold_in(_tk, 500 + 14), (12500, 128), jnp.float32)
        tbl_15 = 0.05 * jax.random.normal(jax.random.fold_in(_tk, 500 + 15), (12500, 128), jnp.float32)
        tbl_16 = 0.05 * jax.random.normal(jax.random.fold_in(_tk, 500 + 16), (1250, 128), jnp.float32)
        tbl_17 = 0.05 * jax.random.normal(jax.random.fold_in(_tk, 500 + 17), (12500, 128), jnp.float32)
        tbl_18 = 0.05 * jax.random.normal(jax.random.fold_in(_tk, 500 + 18), (12500, 128), jnp.float32)
        tbl_19 = 0.05 * jax.random.normal(jax.random.fold_in(_tk, 500 + 19), (1000, 128), jnp.float32)
        tbl_20 = 0.05 * jax.random.normal(jax.random.fold_in(_tk, 500 + 20), (1250, 128), jnp.float32)
        tbl_21 = 0.05 * jax.random.normal(jax.random.fold_in(_tk, 500 + 21), (1000, 128), jnp.float32)
        tbl_22 = 0.05 * jax.random.normal(jax.random.fold_in(_tk, 500 + 22), (1250, 128), jnp.float32)
        tbl_23 = 0.05 * jax.random.normal(jax.random.fold_in(_tk, 500 + 23), (1000, 128), jnp.float32)
        tbl_24 = 0.05 * jax.random.normal(jax.random.fold_in(_tk, 500 + 24), (1250, 128), jnp.float32)
        tbl_25 = 0.05 * jax.random.normal(jax.random.fold_in(_tk, 500 + 25), (1000, 128), jnp.float32)
        _rk = jax.random.fold_in(_tk, 7)
        r_dense_proj = -0.000520686 + 1.00062 * jax.random.normal(jax.random.fold_in(_rk, 101), (512, 128), jnp.float32)
        W_top1 = 0.0405887 * jax.random.normal(jax.random.fold_in(_tk, 801), (607, 512), jnp.float32)
        W_top2 = 0.0441942 * jax.random.normal(jax.random.fold_in(_tk, 802), (512, 256), jnp.float32)
        W_top3 = 0.0625 * jax.random.normal(jax.random.fold_in(_tk, 803), (256, 1), jnp.float32)
        b_top1 = jnp.zeros((512,), jnp.float32)
        b_top2 = jnp.zeros((256,), jnp.float32)
        return (r_dense_proj, ids, tbl_0, tbl_1, tbl_2, tbl_3, tbl_4, tbl_5, tbl_6, tbl_7, tbl_8, tbl_9, tbl_10, tbl_11, tbl_12, tbl_13, tbl_14, tbl_15, tbl_16, tbl_17, tbl_18, tbl_19, tbl_20, tbl_21, tbl_22, tbl_23, tbl_24, tbl_25, W_top1, b_top1, W_top2, b_top2, W_top3)
    r_dense_proj, ids, tbl_0, tbl_1, tbl_2, tbl_3, tbl_4, tbl_5, tbl_6, tbl_7, tbl_8, tbl_9, tbl_10, tbl_11, tbl_12, tbl_13, tbl_14, tbl_15, tbl_16, tbl_17, tbl_18, tbl_19, tbl_20, tbl_21, tbl_22, tbl_23, tbl_24, tbl_25, W_top1, b_top1, W_top2, b_top2, W_top3 = _rec_inputs()

    def _L0_rec_setup():
        import jax, jax.numpy as jnp
        import numpy as np
        key = jax.random.key(seed)
        k1, k2 = jax.random.split(key)
        B, N_SPARSE, D = (2048, 26, 128)
        dense_proj = jax.random.normal(k1, (B, D), dtype=jnp.float32)
        sparse_embs = jax.random.normal(k2, (B, N_SPARSE, D), dtype=jnp.float32)
        return {'dense_proj': dense_proj, 'sparse_embs': sparse_embs}
    _L0_rec_all = _L0_rec_setup()
    _L0_rec_in = {k: v for k, v in _L0_rec_all.items() if k in ()}
    del _L0_rec_all
    return {'r_dense_proj': r_dense_proj, 'ids': ids, 'tbl_0': tbl_0, 'tbl_1': tbl_1, 'tbl_2': tbl_2, 'tbl_3': tbl_3, 'tbl_4': tbl_4, 'tbl_5': tbl_5, 'tbl_6': tbl_6, 'tbl_7': tbl_7, 'tbl_8': tbl_8, 'tbl_9': tbl_9, 'tbl_10': tbl_10, 'tbl_11': tbl_11, 'tbl_12': tbl_12, 'tbl_13': tbl_13, 'tbl_14': tbl_14, 'tbl_15': tbl_15, 'tbl_16': tbl_16, 'tbl_17': tbl_17, 'tbl_18': tbl_18, 'tbl_19': tbl_19, 'tbl_20': tbl_20, 'tbl_21': tbl_21, 'tbl_22': tbl_22, 'tbl_23': tbl_23, 'tbl_24': tbl_24, 'tbl_25': tbl_25, 'W_top1': W_top1, 'b_top1': b_top1, 'W_top2': W_top2, 'b_top2': b_top2, 'W_top3': W_top3}

def reference(r_dense_proj, ids, tbl_0, tbl_1, tbl_2, tbl_3, tbl_4, tbl_5, tbl_6, tbl_7, tbl_8, tbl_9, tbl_10, tbl_11, tbl_12, tbl_13, tbl_14, tbl_15, tbl_16, tbl_17, tbl_18, tbl_19, tbl_20, tbl_21, tbl_22, tbl_23, tbl_24, tbl_25, W_top1, b_top1, W_top2, b_top2, W_top3):
    import jax
    import jax.numpy as jnp

    def _L0_rec_ref(dense_proj, sparse_embs):
        import jax, jax.numpy as jnp
        import numpy as np
        all_vecs = jnp.concatenate([dense_proj[:, None, :], sparse_embs], axis=1)
        n = all_vecs.shape[1]
        interactions = jnp.einsum('bnd,bmd->bnm', all_vecs, all_vecs)
        rows, cols = np.triu_indices(n, k=1)
        interact_flat = interactions[:, rows, cols]
        return jnp.concatenate([dense_proj, interact_flat], axis=1)
    e = jnp.stack([tbl_0[ids[:, 0]], tbl_1[ids[:, 1]], tbl_2[ids[:, 2]], tbl_3[ids[:, 3]], tbl_4[ids[:, 4]], tbl_5[ids[:, 5]], tbl_6[ids[:, 6]], tbl_7[ids[:, 7]], tbl_8[ids[:, 8]], tbl_9[ids[:, 9]], tbl_10[ids[:, 10]], tbl_11[ids[:, 11]], tbl_12[ids[:, 12]], tbl_13[ids[:, 13]], tbl_14[ids[:, 14]], tbl_15[ids[:, 15]], tbl_16[ids[:, 16]], tbl_17[ids[:, 17]], tbl_18[ids[:, 18]], tbl_19[ids[:, 19]], tbl_20[ids[:, 20]], tbl_21[ids[:, 21]], tbl_22[ids[:, 22]], tbl_23[ids[:, 23]], tbl_24[ids[:, 24]], tbl_25[ids[:, 25]]], axis=1)
    z = _L0_rec_ref(r_dense_proj, e)
    z = z.reshape(z.shape[0], -1)
    h = jnp.concatenate([z, r_dense_proj], axis=1)
    h = jnp.maximum(h @ W_top1 + b_top1, 0.0)
    h = jnp.maximum(h @ W_top2 + b_top2, 0.0)
    y = h @ W_top3
    return y

_drawn_inputs = setup_inputs


def setup_inputs(seed=0):
    import zlib

    import numpy as np

    out = dict(_drawn_inputs(seed))
    spreads = {'b_top1': (0.0, 0.1), 'b_top2': (0.0, 0.1)}
    factors = {}
    for name, (base, spread) in spreads.items():
        noise = np.random.default_rng([zlib.crc32(name.encode()), seed]).standard_normal(out[name].shape)
        drawn = base * np.exp(spread * noise) if base else spread * noise
        out[name] = jnp.asarray(drawn.astype(out[name].dtype))
    for name, factor in factors.items():
        out[name] = (out[name] * factor).astype(out[name].dtype)
    return out
```

```python
from contextlib import ExitStack

import concourse.bass as bass
from concourse import mybir

F32 = mybir.dt.float32
F32R = mybir.dt.float32r
I32 = mybir.dt.int32
ALU = mybir.AluOpType
ACT = mybir.ActivationFunctionType

P = 128
TILES = 4
D = 128
FEATURES = 26
VECS = FEATURES + 1
S = 4
QUAD = P // S
GROUPS = P // S
MOVE = VECS + 1
HID1, HID2 = 512, 256

BATCH = 4
BATCHES = [0, 9, 13, 17]
ONEHOT = [f for f in range(FEATURES) if not any(b <= f < b + BATCH for b in BATCHES)]
NB = len(BATCHES)
GSLOTS = 4

KT = -(-VECS // S)
CWIDTH = [min(KT, VECS - KT * c) for c in range(S)]
PAIRS_PER_TILE = 4
GPB = 4

ONE_ROW = VECS


def steps():
    out = [("dense",)]
    feeds = [("batch", t, i) for t in range(TILES) for i in range(NB)]
    hots = [("onehot", o) for o in range(len(ONEHOT))]
    gather_us, hot_us, start_us = 1.04 * BATCH, 4.3, 7.0
    clock, n = start_us, 0
    for h in hots:
        while n < len(feeds) and 6 + gather_us * (n + 1) < clock:
            out.append(feeds[n])
            n += 1
        out.append(h)
        clock += hot_us
    for t in range(TILES):
        while n < len(feeds) and feeds[n][1] <= t:
            out.append(feeds[n])
            n += 1
        if t >= 1:
            out += [("gram", t, 0), ("l1", t - 1), ("gram", t, 1), ("h1t", t - 1), ("gram", t, 2),
                    ("l2", t - 1), ("gram", t, 3)]
        else:
            out += [("gram", t, u) for u in range(PAIRS_PER_TILE)]
    t = TILES - 1
    out += [("l1", t), ("h1t", t), ("l2", t)]
    return out


STEPS = steps()


def fill_list():
    return [s for s in STEPS if s[0] in ("dense", "onehot", "batch")]


FILLS = fill_list()
FILL_OF = {s: i for i, s in enumerate(FILLS)}
LAST_FILL = [max(i for i, s in enumerate(FILLS) if s[0] != "batch" or s[1] == t) for t in range(TILES)]


def build(nc, ins, out):
    ids, ids_t = ins["ids"], ins["ids_t"]
    tables = [ins[f"tbl_{f}"] for f in range(FEATURES)]
    W1, b1, W2, b2, W3 = (ins[n] for n in ("W_top1", "b_top1", "W_top2", "b_top2", "W_top3"))
    NPAIRS = VECS * (VECS - 1) // 2
    rows_of = [tables[f].shape[0] for f in ONEHOT]
    HP = 125
    kts = [r // HP for r in rows_of]
    HK = 5
    assert all(r == HP * k and k % 2 == 0 and k // 2 <= HK for r, k in zip(rows_of, kts))
    NH = len(ONEHOT)

    with ExitStack() as ctx:
        def sb(name, shape, dt):
            return ctx.enter_context(nc.sbuf_tensor(name, shape, dt))

        def sem(name):
            return ctx.enter_context(nc.semaphore(name))

        vec_half = sb("vec_half", [P, TILES, P, QUAD], F32R)
        vec_lo = sb("vec_lo", [P, TILES, P, MOVE], F32R)
        dense_lo_half = sb("dense_lo_half", [P, TILES, P], F32R)
        gathered = sb("gathered", [P, GSLOTS, BATCH, D], F32)
        dense = gathered[:, 1, :, :]
        w2_raw = gathered[:, 2:4, :, :].rearrange("p a b d -> p (a b d)").rearrange("p (k n) -> p k n", n=HID2)
        ids_sb = sb("ids_sb", [P, TILES, FEATURES], I32)
        ident = sb("ident", [P, P], F32)
        row_id = sb("row_id", [P, 2, 2 * HK], F32)
        row_id_i = sb("row_id_i", [P, 2, 2 * HK], I32)
        region = sb("region", [P, 2 * (KT + 1) * HID1], F32R)
        w1_hi = region[:, 0:(KT + 1) * HID1].rearrange("p (k n) -> p k n", n=HID1)
        w1_lo = region[:, (KT + 1) * HID1:].rearrange("p (k n) -> p k n", n=HID1)
        half = 2 * HK * D
        tab_hi = region[:, 0:half].rearrange("p (r k d) -> p r k d", r=2, d=D)
        tab_lo = region[:, half:2 * half].rearrange("p (r k d) -> p r k d", r=2, d=D)
        hot = region[:, 2 * half:2 * half + 2 * HK * HID1].rearrange("p (r k b) -> p r k b", r=2, k=HK)
        stage = sb("stage", [P, KT * HID1], F32)
        tab_raw = stage[:, 0:4 * HK * D].rearrange("p (r c) -> p r c", r=2)
        ids_bc = stage[:, 4 * HK * D:4 * HK * D + 2 * TILES * P].bitcast(I32).rearrange("p (r b) -> p r b", r=2)
        w1_raw = stage[:, :].rearrange("p (k n) -> p k n", n=HID1)
        picked = sb("picked", [P, GROUPS * VECS], F32)
        own = picked[:, :].rearrange("p (g m) -> p g m", g=GROUPS)
        w1_dense = picked[:, 0:HID1]
        w2_hi = sb("w2_hi", [P, 4, HID2], F32R)
        w2_lo = sb("w2_lo", [P, 4, HID2], F32R)
        b2_sb = sb("b2_sb", [1, HID2], F32)
        ones = sb("ones", [1, P], F32)
        w3_bc = sb("w3_bc", [P, HID2], F32)
        prod = sb("prod", [P, KT, P], F32)
        prod_hi = sb("prod_hi", [P, KT, P], F32R)
        prod_lo = sb("prod_lo", [P, KT, P], F32R)
        h1 = sb("h1", [P, HID1], F32)
        w1_second = h1[:, :]
        h1t_hi = sb("h1t_hi", [P, 4, P], F32R)
        h1t_lo = sb("h1t_lo", [P, 4, P], F32R)
        y = sb("y", [P, TILES], F32)

        fill_ps = ctx.enter_context(nc.psum_tensor("fill_ps", [P, 2, 512], F32))
        gram_ps = ctx.enter_context(nc.psum_tensor("gram_ps", [P, 2, 2, 512], F32))
        mlp_ps = ctx.enter_context(nc.psum_tensor("mlp_ps", [P, 512], F32))
        h1t_ps = ctx.enter_context(nc.psum_tensor("h1t_ps", [P, 4, P], F32))

        ids_landed = sem("ids_landed")
        dense_landed = sem("dense_landed")
        w2_landed = sem("w2_landed")
        b2_landed = sem("b2_landed")
        dense_w1_landed = sem("dense_w1_landed")
        w3_landed = sem("w3_landed")
        w1_landed = sem("w1_landed")
        table_landed = [sem(f"table_landed{i}") for i in range(2)]
        bc_landed = [sem(f"bc_landed{i}") for i in range(2)]
        batch_landed = [sem(f"batch_landed{i}") for i in range(GSLOTS)]
        ident_zeroed = sem("ident_zeroed")
        ident_made = sem("ident_made")
        row_ids_made = sem("row_ids_made")
        row_ids_cast = sem("row_ids_cast")
        pads_zeroed = sem("pads_zeroed")
        prod_zeroed = sem("prod_zeroed")
        ones_row_set = sem("ones_row_set")
        dense_lo_halved = sem("dense_lo_halved")
        tab_hi_made = sem("tab_hi_made")
        tab_lo_made = sem("tab_lo_made")
        hot_made = sem("hot_made")
        first_half_used = sem("first_half_used")
        fill_made = sem("fill_made")
        fill_hi_made = sem("fill_hi_made")
        fill_lo_made = sem("fill_lo_made")
        gram_made = sem("gram_made")
        gram_picked = sem("gram_picked")
        prod_packed = sem("prod_packed")
        prod_hi_made = sem("prod_hi_made")
        prod_lo_made = sem("prod_lo_made")
        w1_summed = sem("w1_summed")
        w1_hi_made = sem("w1_hi_made")
        w1_lo_made = sem("w1_lo_made")
        ones_set = sem("ones_set")
        w2_hi_made = sem("w2_hi_made")
        w2_lo_made = sem("w2_lo_made")
        l1_made = sem("l1_made")
        h1_made = sem("h1_made")
        h1t_made = sem("h1t_made")
        h1t_hi_made = sem("h1t_hi_made")
        h1t_lo_made = sem("h1t_lo_made")
        l2_made = sem("l2_made")
        y_made = sem("y_made")
        out_written = sem("out_written")

        def place(vec, step):
            if step[0] == "batch":
                n0 = BATCHES[step[2]] + 1
                return vec[:, step[1], :, n0:n0 + BATCH].rearrange("p q n -> p n q")
            return vec[:, :, :, 0 if step[0] == "dense" else ONEHOT[step[1]] + 1]

        def fill_in(step, bank):
            if step[0] == "onehot":
                return fill_ps[:, bank, :].rearrange("p (q t) -> p t q", t=TILES)
            return fill_ps[:, bank, :].rearrange("p (a q) -> p a q", q=P)

        def wait_half_used(eng, o, h):
            if h == 0:
                eng.wait_ge(first_half_used, o + 1)
            else:
                eng.wait_ge(fill_made, FILL_OF[("onehot", o)] + 1)

        block = ctx.enter_context(nc.Block())

        @block.sync
        def _(sp):
            sp.dma_start(ids_sb[:], ids.rearrange("(q t) f -> q t f", t=TILES)).then_inc(ids_landed, 16)

            def load_table(o):
                f, k = ONEHOT[o], kts[o]
                if o >= 2:
                    sp.wait_ge(hot_made, 2 * (o - 1))
                sp.dma_start(ids_bc[:, o % 2, :],
                             ids_t[f:f + 1, :].to_broadcast([P, TILES * P])).then_inc(bc_landed[o % 2], 16)
                if o >= 2:
                    sp.wait_ge(tab_lo_made, 2 * (o - 1))
                src = tables[f].rearrange("(p k) d -> p (k d)", k=k)
                for a, b in ((0, 112), (112, HP)):
                    sp.dma_start(tab_raw[a:b, o % 2, 0:k * D], src[a:b, :]).then_inc(table_landed[o % 2], 16)

            load_table(0)
            sp.dma_start(dense, ins["r_dense_proj"].rearrange("(q t) d -> q t d", t=TILES)) \
                .then_inc(dense_landed, 16)
            sp.dma_start(w2_raw, W2.rearrange("(k p) n -> p k n", p=P)).then_inc(w2_landed, 16)
            load_table(1)
            sp.dma_start(b2_sb[:], b2.rearrange("(a n) -> a n", a=1)).then_inc(b2_landed, 16)
            sp.dma_start(w1_dense, W1[0:D, :]).then_inc(dense_w1_landed, 16)
            sp.dma_start(w1_second, W1[D + NPAIRS:D + NPAIRS + D, :]).then_inc(dense_w1_landed, 16)
            sp.dma_start(w3_bc[:], W3.rearrange("n o -> o n").to_broadcast([P, HID2])).then_inc(w3_landed, 16)
            for o in range(2, NH):
                load_table(o)
            sp.wait_ge(hot_made, 2 * NH)
            sp.wait_ge(tab_lo_made, 2 * NH)
            sp.dma_start(w1_raw, ins["w1_pairs"].rearrange("k p n -> p k n")).then_inc(w1_landed, 16)
            sp.wait_ge(y_made, TILES)
            sp.dma_start(out.rearrange("(q t) o -> q (t o)", t=TILES), y[:]).then_inc(out_written, 16)
            sp.wait_ge(out_written, 16)

        @block.gpsimd
        def _(pool):
            nc.gpsimd.memset(ident[:], 0.0).then_inc(ident_zeroed, 1)
            nc.gpsimd.memset(prod[:], 0.0).then_inc(prod_zeroed, 1)
            nc.gpsimd.memset(vec_lo[:, :, :, VECS:MOVE].bitcast(F32), 0.0).then_inc(pads_zeroed, 1)
            nc.gpsimd.iota(row_id_i[:, 0, :], pattern=[[1, 2 * HK]], base=0, channel_multiplier=8)
            nc.gpsimd.iota(row_id_i[:, 1, :], pattern=[[1, 2 * HK]], base=0, channel_multiplier=10) \
                .then_inc(row_ids_made, 1)
            pool.wait_ge(ident_zeroed, 1)
            nc.gpsimd.affine_select(out=ident[:], in_=ident[:], compare_op=ALU.not_equal, fill=1.0, base=0,
                                    pattern=[[-1, P]], channel_multiplier=1).then_inc(ident_made, 1)
            pool.wait_ge(ids_landed, 16)
            for t in range(TILES):
                for i in range(NB):
                    n = t * NB + i
                    if n == 1:
                        pool.wait_ge(fill_made, FILL_OF[("dense",)] + 1)
                    if n == 2:
                        pool.wait_ge(w2_lo_made, 1)
                    if n >= GSLOTS:
                        old = n - GSLOTS
                        pool.wait_ge(fill_made, FILL_OF[("batch", old // NB, old % NB)] + 1)
                    for j in range(BATCH):
                        f = BATCHES[i] + j
                        pool.indirect_dma_start(
                            out=gathered[:, n % GSLOTS, j, :], out_offset=None, in_=tables[f],
                            in_offset=bass.IndirectOffsetOnAxis(ap=ids_sb[:, t, f:f + 1], axis=0),
                        ).then_inc(batch_landed[n % GSLOTS], 16)

        @block.scalar
        def _(act):
            def split_half(o, h):
                c, k = 2 * o + h, kts[o] // 2
                act.wait_ge(table_landed[o % 2], 32 * (o // 2 + 1))
                if o >= 1:
                    wait_half_used(act, o - 1, h)
                src = tab_raw[0:HP, o % 2, h * k * D:(h + 1) * k * D].rearrange("p (k d) -> p k d", d=D)
                nc.scalar.copy(tab_hi[0:HP, c % 2, 0:k, :], src).then_inc(tab_hi_made, 1)

            split_half(0, 0)
            split_half(0, 1)
            act.wait_ge(w2_landed, 16)
            nc.scalar.copy(w2_hi[:], w2_raw).then_inc(w2_hi_made, 1)
            for step in STEPS:
                kind = step[0]
                if kind in ("dense", "onehot", "batch"):
                    if kind == "onehot" and step[1] + 1 < NH:
                        split_half(step[1] + 1, 0)
                    i = FILL_OF[step]
                    act.wait_ge(fill_made, i + 1)
                    nc.scalar.mul(place(vec_half, step), fill_in(step, i % 2), 0.5).then_inc(fill_hi_made, 1)
                    if kind == "onehot" and step[1] + 1 < NH:
                        split_half(step[1] + 1, 1)
                    if kind == "onehot" and step[1] == NH - 1:
                        wait_half_used(act, NH - 1, 1)
                        act.wait_ge(w1_summed, 1)
                        nc.scalar.mul(w1_hi[:, KT, :], w1_dense, 2.0).then_inc(w1_hi_made, 1)
                        act.wait_ge(w1_landed, 16)
                        nc.scalar.copy(w1_hi[:, 0:KT, :], w1_raw).then_inc(w1_hi_made, 1)
                elif kind == "gram":
                    _, t, u = step
                    i = PAIRS_PER_TILE * t + u
                    act.wait_ge(gram_made, i + 1)
                    if i == 0:
                        act.wait_ge(w1_lo_made, 1)
                    if t >= 1 and u == 0:
                        act.wait_ge(prod_packed, t)
                    for s in range(S):
                        src = gram_ps[QUAD * s:QUAD * s + VECS, i % 2, :, 0:GPB * S * MOVE] \
                            .rearrange("p b (g a) -> p b g a", g=GPB)[:, :, :, s * MOVE:s * MOVE + VECS]
                        dst = own[QUAD * s:QUAD * s + VECS, 2 * GPB * u:2 * GPB * (u + 1), :] \
                            .rearrange("p (b g) m -> p b g m", b=2)
                        last = nc.scalar.mul(dst, src, 2.0)
                    last.then_inc(gram_picked, 1)
                    if u == PAIRS_PER_TILE - 1:
                        act.wait_ge(prod_packed, t + 1)
                        if t >= 1:
                            act.wait_ge(l1_made, t)
                        nc.scalar.copy(prod_hi[:], prod[:]).then_inc(prod_hi_made, 1)
                elif kind == "l1":
                    t = step[1]
                    act.wait_ge(l1_made, t + 1)
                    if t >= 1:
                        act.wait_ge(h1t_made, t)
                    nc.scalar.activation(h1[:], mlp_ps[:], ACT.Relu).then_inc(h1_made, 1)
                elif kind == "h1t":
                    t = step[1]
                    act.wait_ge(h1t_made, t + 1)
                    if t >= 1:
                        act.wait_ge(l2_made, t)
                    nc.scalar.copy(h1t_hi[:], h1t_ps[:]).then_inc(h1t_hi_made, 1)

        @block.vector
        def _(dve):
            nc.vector.memset(ones[:], 1.0).then_inc(ones_set, 1)
            nc.vector.memset(vec_half[:, :, :, VECS:QUAD].bitcast(F32), 0.0).then_inc(pads_zeroed, 1)
            dve.wait_ge(prod_zeroed, 1)
            nc.vector.memset(prod[0:QUAD, 0, :], 1.0).then_inc(ones_row_set, 1)
            dve.wait_ge(row_ids_made, 1)
            nc.vector.tensor_copy(row_id[:], row_id_i[:]).then_inc(row_ids_cast, 1)

            def split_half(o, h):
                c, k = 2 * o + h, kts[o] // 2
                dve.wait_ge(row_ids_cast, 1)
                dve.wait_ge(bc_landed[o % 2], 16 * (o // 2 + 1))
                if o >= 1:
                    wait_half_used(dve, o - 1, h)
                for j in range(k):
                    last = nc.vector.tensor_scalar(hot[0:HP, c % 2, j, :], ids_bc[0:HP, o % 2, :],
                                                   row_id[0:HP, (kts[o] - 8) // 2, h * k + j:h * k + j + 1],
                                                   None, ALU.is_equal)
                last.then_inc(hot_made, 1)
                dve.wait_ge(tab_hi_made, c + 1)
                src = tab_raw[0:HP, o % 2, h * k * D:(h + 1) * k * D].rearrange("p (k d) -> p k d", d=D)
                nc.vector.tensor_tensor(tab_lo[0:HP, c % 2, 0:k, :], src,
                                        tab_hi[0:HP, c % 2, 0:k, :].bitcast(F32), ALU.subtract) \
                    .then_inc(tab_lo_made, 1)

            split_half(0, 0)
            split_half(0, 1)
            dve.wait_ge(w2_hi_made, 1)
            nc.vector.tensor_tensor(w2_lo[:], w2_raw, w2_hi[:].bitcast(F32), ALU.subtract).then_inc(w2_lo_made, 1)
            for step in STEPS:
                kind = step[0]
                if kind in ("dense", "onehot", "batch"):
                    if kind == "onehot" and step[1] + 1 < NH:
                        split_half(step[1] + 1, 0)
                    i = FILL_OF[step]
                    dve.wait_ge(fill_hi_made, i + 1)
                    nc.vector.scalar_tensor_tensor(
                        out=place(vec_lo, step), in0=place(vec_half, step).bitcast(F32), scalar=-2.0,
                        in1=fill_in(step, i % 2), op0=ALU.mult, op1=ALU.add).then_inc(fill_lo_made, 1)
                    if kind == "dense":
                        dve.wait_ge(fill_lo_made, i + 1)
                        nc.vector.tensor_scalar(dense_lo_half[:], place(vec_lo, step).bitcast(F32), 0.5, None,
                                                ALU.mult).then_inc(dense_lo_halved, 1)
                    if kind == "onehot" and step[1] + 1 < NH:
                        split_half(step[1] + 1, 1)
                    if kind == "onehot" and step[1] == NH - 1:
                        dve.wait_ge(dense_w1_landed, 32)
                        nc.vector.tensor_tensor(w1_dense, w1_dense, w1_second, ALU.add).then_inc(w1_summed, 1)
                        dve.wait_ge(w1_summed, 1)
                        dve.wait_ge(w1_hi_made, 1)
                        nc.vector.scalar_tensor_tensor(out=w1_lo[:, KT, :], in0=w1_dense, scalar=2.0,
                                                       in1=w1_hi[:, KT, :].bitcast(F32),
                                                       op0=ALU.mult, op1=ALU.subtract)
                        dve.wait_ge(w1_hi_made, 2)
                        nc.vector.tensor_tensor(w1_lo[:, 0:KT, :], w1_raw, w1_hi[:, 0:KT, :].bitcast(F32),
                                                ALU.subtract).then_inc(w1_lo_made, 1)
                elif kind == "gram" and step[2] == PAIRS_PER_TILE - 1:
                    t = step[1]
                    if t == 0:
                        dve.wait_ge(ones_row_set, 1)
                    else:
                        dve.wait_ge(prod_hi_made, t)
                        dve.wait_ge(prod_lo_made, t)
                    dve.wait_ge(gram_picked, PAIRS_PER_TILE * (t + 1))
                    for c in range(S):
                        for s in range(S):
                            src = own[QUAD * s:QUAD * s + VECS, :, KT * c:KT * c + CWIDTH[c]] \
                                .rearrange("p g m -> p m g")
                            dst = prod[QUAD * c:QUAD * c + VECS, 0:CWIDTH[c], :] \
                                .rearrange("p j (g s) -> p j g s", s=S)[:, :, :, s]
                            last = nc.vector.tensor_copy(dst, src)
                    last.then_inc(prod_packed, 1)
                    dve.wait_ge(prod_hi_made, t + 1)
                    if t >= 1:
                        dve.wait_ge(l1_made, t)
                    nc.vector.tensor_tensor(prod_lo[:], prod[:], prod_hi[:].bitcast(F32), ALU.subtract) \
                        .then_inc(prod_lo_made, 1)
                elif kind == "h1t":
                    t = step[1]
                    dve.wait_ge(h1t_hi_made, t + 1)
                    if t >= 1:
                        dve.wait_ge(l2_made, t)
                    nc.vector.tensor_tensor(h1t_lo[:], h1t_ps[:], h1t_hi[:].bitcast(F32), ALU.subtract) \
                        .then_inc(h1t_lo_made, 1)
                elif kind == "l2":
                    t = step[1]
                    dve.wait_ge(l2_made, t + 1)
                    if t == 0:
                        dve.wait_ge(w3_landed, 16)
                    else:
                        dve.wait_ge(y_made, t)
                    nc.vector.scalar_tensor_tensor(out=mlp_ps[:, 0:HID2], in0=mlp_ps[:, 0:HID2], scalar=0.0, in1=w3_bc[:],
                                                   op0=ALU.max, op1=ALU.mult, accum_out=y[:, t:t + 1]) \
                        .then_inc(y_made, 1)

        @block.tensor
        def _(pe):
            for step in STEPS:
                kind = step[0]
                if kind in ("dense", "onehot", "batch"):
                    i = FILL_OF[step]
                    if i >= 2:
                        pe.wait_ge(fill_lo_made, i - 1)
                    if kind == "onehot":
                        o = step[1]
                        for h in range(2):
                            c, k = 2 * o + h, kts[o] // 2
                            pe.wait_ge(hot_made, c + 1)
                            pe.wait_ge(tab_lo_made, c + 1)
                            for j in range(k):
                                for part in (tab_hi, tab_lo):
                                    last = nc.tensor.matmul(fill_ps[:, i % 2, :], part[0:HP, c % 2, j, :],
                                                            hot[0:HP, c % 2, j, :],
                                                            start=(h == 0 and j == 0 and part is tab_hi),
                                                            stop=(h == 1 and j == k - 1 and part is tab_lo))
                            last.then_inc(first_half_used if h == 0 else fill_made, 1)
                        continue
                    if kind == "dense":
                        pe.wait_ge(ident_made, 1)
                        pe.wait_ge(dense_landed, 16)
                    else:
                        n = step[1] * NB + step[2]
                        pe.wait_ge(batch_landed[n % GSLOTS], 16 * BATCH * (n // GSLOTS + 1))
                    for j in range(4):
                        src = dense[:, j, :] if kind == "dense" else gathered[:, n % GSLOTS, j, :]
                        last = nc.tensor.transpose(fill_ps[:, i % 2, j * P:(j + 1) * P], src, ident[:])
                    last.then_inc(fill_made, 1)
                elif kind == "gram":
                    _, t, u = step
                    i = PAIRS_PER_TILE * t + u
                    if u == 0:
                        pe.wait_ge(fill_lo_made, LAST_FILL[t] + 1)
                        pe.wait_ge(pads_zeroed, 2)
                    if i >= 2:
                        pe.wait_ge(gram_picked, i - 1)
                    for b in range(2):
                        for gb in range(GPB):
                            q0 = S * (2 * GPB * u + GPB * b + gb)
                            o = gram_ps[:, i % 2, b, gb * S * MOVE:(gb + 1) * S * MOVE]
                            still = vec_half[:, t, q0:q0 + S, :].rearrange("p q n -> p (q n)")
                            nc.tensor.matmul(o, still, vec_half[:, t, q0:q0 + S, 0:MOVE], start=True, stop=False)
                            last = nc.tensor.matmul(o, still, vec_lo[:, t, q0:q0 + S, :], start=False, stop=True)
                    last.then_inc(gram_made, 1)
                elif kind == "l1":
                    t = step[1]
                    pe.wait_ge(w1_lo_made, 1)
                    pe.wait_ge(dense_lo_halved, 1)
                    pe.wait_ge(prod_lo_made, t + 1)
                    if t >= 1:
                        pe.wait_ge(y_made, t)
                    for k in [KT] + list(range(KT)):
                        if k == KT:
                            hi, lo = vec_half[:, t, :, 0], dense_lo_half[:, t, :]
                        else:
                            hi, lo = prod_hi[:, k, :], prod_lo[:, k, :]
                        nc.tensor.matmul(mlp_ps[:], hi, w1_hi[:, k, :], start=(k == KT), stop=False)
                        nc.tensor.matmul(mlp_ps[:], hi, w1_lo[:, k, :], start=False, stop=False)
                        last = nc.tensor.matmul(mlp_ps[:], lo, w1_hi[:, k, :], start=False, stop=(k == KT - 1))
                    last.then_inc(l1_made, 1)
                elif kind == "h1t":
                    t = step[1]
                    pe.wait_ge(h1_made, t + 1)
                    if t >= 1:
                        pe.wait_ge(h1t_lo_made, t)
                    for k in range(4):
                        last = nc.tensor.transpose(h1t_ps[:, k, :], h1[:, k * P:(k + 1) * P], ident[:])
                    last.then_inc(h1t_made, 1)
                elif kind == "l2":
                    t = step[1]
                    pe.wait_ge(w2_lo_made, 1)
                    pe.wait_ge(h1t_lo_made, t + 1)
                    o = mlp_ps[:, 0:HID2]
                    pe.wait_ge(b2_landed, 16)
                    pe.wait_ge(ones_set, 1)
                    nc.tensor.matmul(o, ones[:], b2_sb[:], start=True, stop=False)
                    for k in range(4):
                        nc.tensor.matmul(o, h1t_hi[:, k, :], w2_hi[:, k, :], start=False, stop=False)
                        nc.tensor.matmul(o, h1t_hi[:, k, :], w2_lo[:, k, :], start=False, stop=False)
                        last = nc.tensor.matmul(o, h1t_lo[:, k, :], w2_hi[:, k, :], start=False, stop=(k == 3))
                    last.then_inc(l2_made, 1)


def pair_rows(np, w1, b1):
    laid = np.zeros((KT, P, w1.shape[1]), w1.dtype)
    row = D
    for n in range(VECS):
        for m in range(n + 1, VECS):
            laid[m % KT, QUAD * (m // KT) + n] = w1[row]
            laid[n % KT, QUAD * (n // KT) + m] = w1[row]
            row += 1
    laid[0, ONE_ROW] = b1
    return laid


def kernel(**inputs):
    import numpy as np
    import concourse.bacc as bacc
    from concourse.bass_utils import run_bass_kernel_spmd as run

    nc = bacc.Bacc("TRN2", target_bir_lowering=False, num_devices=1)
    arrays, aps = {}, {}
    laid_out = {name: np.ascontiguousarray(a) for name, a in inputs.items()}
    laid_out["ids_t"] = np.ascontiguousarray(laid_out["ids"].T)
    laid_out["w1_pairs"] = pair_rows(np, laid_out["W_top1"], laid_out["b_top1"])
    for name, a in laid_out.items():
        arrays[f"in_{name}"] = a
        aps[name] = nc.dram_tensor(f"in_{name}", a.shape, mybir.dt.from_np(a.dtype), kind="ExternalInput").ap()
    out = nc.dram_tensor("out_y", (512, 1), F32, kind="ExternalOutput").ap()
    build(nc, aps, out)
    r = run(nc, [arrays], core_ids=[0])
    return r.results[0]["out_y"]
```

```python
from contextlib import ExitStack

import concourse.bass as bass
from concourse import mybir

F32 = mybir.dt.float32
F32R = mybir.dt.float32r
I32 = mybir.dt.int32
ALU = mybir.AluOpType
ACT = mybir.ActivationFunctionType

P = 128
TILES = 4
D = 128
FEATURES = 26
VECS = FEATURES + 1
NPAIRS = VECS * (VECS - 1) // 2
S = 4
QUAD = P // S
COLS = VECS - 1
GPB = 4
PAIRS = 4
GROUPS = 2 * GPB
PAIR_Q = GROUPS * S
HID1, HID2 = 512, 256

BATCHES = [[0, 1, 4, 5], [9, 10, 11, 12], [13, 14, 15, 16], [17, 18, 19, 20], [22, 23, 24]]
ONEHOT = [f for f in range(FEATURES) if not any(f in b for b in BATCHES)]
NB = len(BATCHES)
NH = len(ONEHOT)
GSLOTS = 8
ACT_HOT = 1

HP, HK = 125, 4

KT = -(-COLS // S)
CWIDTH = [min(KT, COLS - KT * c) for c in range(S)]
ONE_ROW = VECS


def order_of_work():
    out = [("dense",)]
    feeds = [("batch", t, i) for t in range(TILES) for i in range(NB)]
    gathers = 0
    for o in range(NH):
        out.append(("onehot", o))
        while feeds and gathers + len(BATCHES[feeds[0][2]]) <= 4 * o + 3:
            gathers += len(BATCHES[feeds[0][2]])
            out.append(feeds.pop(0))
    for t in range(TILES):
        mlp = [("l1", t - 1), ("h1t", t - 1), ("l2", t - 1)] if t else []
        own = [f for f in feeds if f[1] == t]
        feeds = [f for f in feeds if f[1] > t]
        for f in own:
            out.append(f)
        for u in range(PAIRS):
            if u == PAIRS - 1 and feeds and t + 1 < TILES - 1:
                out.append(feeds.pop(0))
            out.append(("gram", t, u))
            if u < PAIRS - 1 and feeds:
                out.append(feeds.pop(0))
            if mlp:
                out.append(mlp.pop(0))
                if u == 0 and feeds:
                    out.append(feeds.pop(0))
    t = TILES - 1
    out += [("l1", t), ("h1t", t), ("l2", t)]
    return out


STEPS = order_of_work()
FILLS = [s for s in STEPS if s[0] in ("dense", "onehot", "batch")]
FILL_OF = {s: i for i, s in enumerate(FILLS)}
LAST_FILL = [max(i for i, s in enumerate(FILLS) if s[0] != "batch" or s[1] == t) for t in range(TILES)]
LAST_HOT = FILL_OF[("onehot", NH - 1)]
BY_DVE = [i > LAST_HOT and i % 2 == 0 for i in range(len(FILLS))]

W1_STEPS = [("onehot", o) for o in range(2, NH)] + [("gram", 0, u) for u in range(PAIRS)]
W1_AFTER = {step: [k for k in range(KT) if k * len(W1_STEPS) // KT == i] for i, step in enumerate(W1_STEPS)}


def build(nc, ins, out):
    tables = [ins[f"tbl_{f}"] for f in range(FEATURES)]
    W1, W2 = ins["W_top1"], ins["W_top2"]
    assert all(tables[f].shape[0] == HP * 2 * HK for f in ONEHOT)

    with ExitStack() as ctx:
        def sb(name, shape, dt):
            return ctx.enter_context(nc.sbuf_tensor(name, shape, dt))

        def sem(name):
            return ctx.enter_context(nc.semaphore(name))

        vec = sb("vec", [P, TILES, P, QUAD], F32)
        gathered = sb("gathered", [P, GSLOTS, 4, D], F32)
        dense = sb("dense", [P, TILES, D], F32)
        ids_sb = sb("ids_sb", [P, TILES, FEATURES], I32)
        ident = sb("ident", [P, P], F32)
        row_id_i = sb("row_id_i", [P, 2 * HK], I32)
        row_id = sb("row_id", [P, 2 * HK], F32)
        minus_row_id = sb("minus_row_id", [P, 2 * HK], F32)
        one_col = sb("one_col", [P, 1], F32)
        tab_raw = sb("tab_raw", [P, 2, 2 * HK * D], F32)
        ids_bc = sb("ids_bc", [P, 2, TILES * P], I32)
        tab_hi = sb("tab_hi", [P, 2, HK, D], F32R)
        tab_lo = sb("tab_lo", [P, 2, HK, D], F32R)
        hot = sb("hot", [P, 2, HK, TILES * P], F32R)
        w1_raw = sb("w1_raw", [P, KT, HID1], F32)
        w1_hi = sb("w1_hi", [P, KT, HID1], F32R)
        w1_lo = sb("w1_lo", [P, KT, HID1], F32R)
        w1_dense = sb("w1_dense", [P, HID1], F32)
        w1_second = sb("w1_second", [P, HID1], F32)
        w2_sb = sb("w2_sb", [P, 4, HID2], F32)
        b2_sb = sb("b2_sb", [1, HID2], F32)
        ones = sb("ones", [1, P], F32)
        w3_bc = sb("w3_bc", [P, HID2], F32)
        prod = sb("prod", [P, 2, KT, PAIR_Q], F32)
        prod_hi = sb("prod_hi", [P, 2, KT, P], F32R)
        prod_lo = sb("prod_lo", [P, 2, KT, P], F32R)
        h1 = sb("h1", [P, HID1], F32)
        h1t = sb("h1t", [P, 4, P], F32)
        y = sb("y", [P, TILES], F32)

        fill_ps = ctx.enter_context(nc.psum_tensor("fill_ps", [P, 2, 512], F32))
        gram_ps = ctx.enter_context(nc.psum_tensor("gram_ps", [P, 2, 2, 512], F32))
        mlp_ps = ctx.enter_context(nc.psum_tensor("mlp_ps", [P, 512], F32))
        h1t_ps = ctx.enter_context(nc.psum_tensor("h1t_ps", [P, 4, P], F32))

        ids_landed = sem("ids_landed")
        dense_landed = sem("dense_landed")
        w1_landed = sem("w1_landed")
        dense_w1_landed = sem("dense_w1_landed")
        w2_landed = sem("w2_landed")
        w3_landed = sem("w3_landed")
        table_landed = [sem(f"table_landed{i}") for i in range(2)]
        bc_landed = [sem(f"bc_landed{i}") for i in range(2)]
        batch_landed = [sem(f"batch_landed{i}") for i in range(GSLOTS)]
        ident_zeroed = sem("ident_zeroed")
        ident_made = sem("ident_made")
        row_ids_made = sem("row_ids_made")
        row_ids_cast = sem("row_ids_cast")
        pads_zeroed = sem("pads_zeroed")
        prod_zeroed = sem("prod_zeroed")
        ones_row_set = sem("ones_row_set")
        ones_set = sem("ones_set")
        tab_hi_made = sem("tab_hi_made")
        tab_lo_made = sem("tab_lo_made")
        distance_made = sem("distance_made")
        hot_made_act = sem("hot_made_act")
        hot_made_dve = sem("hot_made_dve")
        first_half_used = sem("first_half_used")
        fill_made = sem("fill_made")
        fill_copied_act = sem("fill_copied_act")
        fill_copied_dve = sem("fill_copied_dve")
        gram_made = sem("gram_made")
        packed_act = sem("packed_act")
        packed_dve = sem("packed_dve")
        prod_hi_made = sem("prod_hi_made")
        prod_lo_made = sem("prod_lo_made")
        w1_summed = sem("w1_summed")
        w1_hi_made = sem("w1_hi_made")
        w1_lo_made = sem("w1_lo_made")
        l1_made = sem("l1_made")
        h1_made = sem("h1_made")
        h1t_made = sem("h1t_made")
        h1t_copied = sem("h1t_copied")
        l2_made = sem("l2_made")
        y_made = sem("y_made")
        out_written = sem("out_written")

        def fill_copy(copy, step, bank):
            src = fill_ps[:, bank, :]
            if step[0] == "onehot":
                return copy(vec[:, :, :, ONEHOT[step[1]] + 1], src.rearrange("p (q t) -> p t q", t=TILES))
            if step[0] == "dense":
                return copy(vec[:, :, :, 0], src.rearrange("p (t q) -> p t q", t=TILES))
            fs = BATCHES[step[2]]
            n, first, by = len(fs), fs[0] + 1, fs[1] - fs[0]
            slots = vec[:, step[1], :, :]
            if all(b - a == by for a, b in zip(fs, fs[1:])):
                return copy(slots[:, :, first:fs[-1] + 2:by].rearrange("p q n -> p n q"),
                            src[:, 0:n * P].rearrange("p (n q) -> p n q", n=n))
            gap = fs[2] - fs[0]
            assert by == 1 and fs == [fs[0], fs[0] + 1, fs[0] + gap, fs[0] + gap + 1]
            return copy(slots[:, :, first:first + 2 * gap].rearrange("p q (a n) -> p a n q", a=2)[:, :, 0:2, :],
                        src.rearrange("p (a n q) -> p a n q", a=2, n=2))

        def wait_copied(eng, i):
            n = sum(BY_DVE[:i + 1])
            eng.wait_ge(fill_copied_act, i + 1 - n)
            if n:
                eng.wait_ge(fill_copied_dve, n)

        def wait_half_used(eng, o, h):
            if h == 0:
                eng.wait_ge(first_half_used, o + 1)
            else:
                eng.wait_ge(fill_made, FILL_OF[("onehot", o)] + 1)

        def pack(copy, i, quadrants):
            for s in quadrants:
                own = gram_ps[QUAD * s:QUAD * s + VECS, i % 2, :, 0:GPB * S * COLS] \
                    .rearrange("p b (g a) -> p b g a", g=GPB)
                to = prod[:, i % 2, :, :].rearrange("p j (b g s) -> p b g j s", b=2, s=S)
                for c in range(S):
                    m = s * COLS + KT * c
                    last = copy(to[QUAD * c:QUAD * c + VECS, :, :, 0:CWIDTH[c], s],
                                own[:, :, :, m:m + CWIDTH[c]])
            return last

        block = ctx.enter_context(nc.Block())

        @block.sync
        def _(sp):
            def load_table(o):
                f = ONEHOT[o]
                if o >= 2:
                    sp.wait_ge(hot_made_dve, 2 * (o - 1))
                    sp.wait_ge(hot_made_act, 2 * (o - 1))
                sp.dma_start(ids_bc[:, o % 2, :], ins["ids_t"][f:f + 1, :].to_broadcast([P, TILES * P])) \
                    .then_inc(bc_landed[o % 2], 16)
                if o >= 2:
                    sp.wait_ge(tab_lo_made, 2 * (o - 1))
                src = tables[f].rearrange("(p k) d -> p (k d)", p=HP)
                for a, b in ((0, 112), (112, HP)):
                    sp.dma_start(tab_raw[a:b, o % 2, :], src[a:b, :]).then_inc(table_landed[o % 2], 16)

            sp.dma_start(ids_sb[:], ins["ids"].rearrange("(q t) f -> q t f", t=TILES)).then_inc(ids_landed, 16)
            load_table(0)
            sp.dma_start(dense[:], ins["r_dense_proj"].rearrange("(q t) d -> q t d", t=TILES)) \
                .then_inc(dense_landed, 16)
            load_table(1)
            load_table(2)
            sp.dma_start(w1_dense[:], W1[0:D, :]).then_inc(dense_w1_landed, 16)
            sp.dma_start(w1_second[:], W1[D + NPAIRS:D + NPAIRS + D, :]).then_inc(dense_w1_landed, 16)
            load_table(3)
            sp.dma_start(w1_raw[:], ins["w1_pairs"].rearrange("k p n -> p k n")).then_inc(w1_landed, 16)
            load_table(4)
            sp.dma_start(w2_sb[:], W2.rearrange("(k p) n -> p k n", p=P)).then_inc(w2_landed, 16)
            sp.dma_start(b2_sb[:], ins["b_top2"].rearrange("(a n) -> a n", a=1)).then_inc(w2_landed, 16)
            sp.dma_start(w3_bc[:], ins["W_top3"].rearrange("n o -> o n").to_broadcast([P, HID2])) \
                .then_inc(w3_landed, 16)
            for o in range(5, NH):
                load_table(o)
            sp.wait_ge(y_made, TILES)
            sp.dma_start(out.rearrange("(q t) o -> q (t o)", t=TILES), y[:]).then_inc(out_written, 16)
            sp.wait_ge(out_written, 16)

        @block.gpsimd
        def _(pool):
            nc.gpsimd.memset(ident[:], 0.0).then_inc(ident_zeroed, 1)
            nc.gpsimd.iota(row_id_i[:], pattern=[[1, 2 * HK]], base=0, channel_multiplier=2 * HK) \
                .then_inc(row_ids_made, 1)
            pool.wait_ge(ident_zeroed, 1)
            nc.gpsimd.affine_select(out=ident[:], in_=ident[:], compare_op=ALU.not_equal, fill=1.0, base=0,
                                    pattern=[[-1, P]], channel_multiplier=1).then_inc(ident_made, 1)
            nc.gpsimd.memset(prod[:], 0.0).then_inc(prod_zeroed, 1)
            pool.wait_ge(ids_landed, 16)
            for t in range(TILES):
                for i in range(NB):
                    n = t * NB + i
                    if n >= GSLOTS:
                        old = n - GSLOTS
                        pool.wait_ge(fill_made, FILL_OF[("batch", old // NB, old % NB)] + 1)
                    for j, f in enumerate(BATCHES[i]):
                        pool.indirect_dma_start(
                            out=gathered[:, n % GSLOTS, j, :], out_offset=None, in_=tables[f],
                            in_offset=bass.IndirectOffsetOnAxis(ap=ids_sb[:, t, f:f + 1], axis=0),
                        ).then_inc(batch_landed[n % GSLOTS], 16)

        @block.scalar
        def _(act):
            def half_table(o, h):
                c = 2 * o + h
                act.wait_ge(row_ids_cast, 2)
                act.wait_ge(bc_landed[o % 2], 16 * (o // 2 + 1))
                if o >= 1:
                    wait_half_used(act, o - 1, h)
                for j in range(ACT_HOT):
                    k = HK * h + j
                    nc.scalar.activation(hot[0:HP, h, j, :], ids_bc[0:HP, o % 2, :], ACT.Abs,
                                         bias=minus_row_id[0:HP, k:k + 1]).then_inc(distance_made, 1)
                act.wait_ge(table_landed[o % 2], 32 * (o // 2 + 1))
                src = tab_raw[0:HP, o % 2, h * HK * D:(h + 1) * HK * D].rearrange("p (k d) -> p k d", d=D)
                nc.scalar.copy(tab_hi[0:HP, h, :, :], src).then_inc(tab_hi_made, 1)
                act.wait_ge(distance_made, ACT_HOT * (c + 1))
                act.wait_ge(ones_set, 2)
                for j in range(ACT_HOT):
                    last = nc.scalar.activation(hot[0:HP, h, j, :], hot[0:HP, h, j, :].bitcast(F32), ACT.Relu,
                                                bias=one_col[0:HP, :], scale=-1.0)
                last.then_inc(hot_made_act, 1)

            half_table(0, 0)
            half_table(0, 1)
            for step in STEPS:
                kind = step[0]
                if kind in ("dense", "onehot", "batch"):
                    if kind == "onehot" and step[1] + 1 < NH:
                        half_table(step[1] + 1, 0)
                    i = FILL_OF[step]
                    if not BY_DVE[i]:
                        act.wait_ge(fill_made, i + 1)
                        act.wait_ge(pads_zeroed, 1)
                        fill_copy(nc.scalar.copy, step, i % 2).then_inc(fill_copied_act, 1)
                    if kind == "onehot" and step[1] + 1 < NH:
                        half_table(step[1] + 1, 1)
                elif kind == "gram":
                    _, t, u = step
                    i = PAIRS * t + u
                    act.wait_ge(gram_made, i + 1)
                    if i == 0:
                        act.wait_ge(ones_row_set, 1)
                    if i >= 2:
                        act.wait_ge(prod_lo_made, i - 1)
                        act.wait_ge(prod_hi_made, i - 1)
                    pack(nc.scalar.copy, i, (0, 1)).then_inc(packed_act, 1)
                    act.wait_ge(packed_act, i + 1)
                    act.wait_ge(packed_dve, i + 1)
                    if t >= 2:
                        act.wait_ge(l1_made, t - 1)
                    nc.scalar.copy(prod_hi[:, t % 2, :, PAIR_Q * u:PAIR_Q * (u + 1)], prod[:, i % 2, :, :]) \
                        .then_inc(prod_hi_made, 1)
                elif kind == "l1":
                    t = step[1]
                    act.wait_ge(l1_made, t + 1)
                    if t >= 1:
                        act.wait_ge(h1t_made, t)
                    nc.scalar.activation(h1[:], mlp_ps[:], ACT.Relu).then_inc(h1_made, 1)
                elif kind == "h1t":
                    t = step[1]
                    act.wait_ge(h1t_made, t + 1)
                    if t >= 1:
                        act.wait_ge(l2_made, t)
                    nc.scalar.copy(h1t[:], h1t_ps[:]).then_inc(h1t_copied, 1)
                for k in W1_AFTER.get(step, ()):
                    act.wait_ge(w1_landed, 16)
                    nc.scalar.copy(w1_hi[:, k, :], w1_raw[:, k, :]).then_inc(w1_hi_made, 1)

        @block.vector
        def _(dve):
            nc.vector.memset(ones[:], 1.0).then_inc(ones_set, 1)
            nc.vector.memset(one_col[:], 1.0).then_inc(ones_set, 1)
            dve.wait_ge(row_ids_made, 1)
            nc.vector.tensor_copy(row_id[:], row_id_i[:]).then_inc(row_ids_cast, 1)
            nc.vector.tensor_scalar(minus_row_id[:], row_id_i[:], -1.0, None, ALU.mult).then_inc(row_ids_cast, 1)
            nc.vector.memset(vec[:, :, :, VECS:QUAD], 0.0).then_inc(pads_zeroed, 1)
            dve.wait_ge(prod_zeroed, 1)
            nc.vector.memset(prod[0:QUAD, :, 0, :], 1.0).then_inc(ones_row_set, 1)
            dve.wait_ge(row_ids_cast, 2)

            def half_table(o, h):
                c = 2 * o + h
                dve.wait_ge(bc_landed[o % 2], 16 * (o // 2 + 1))
                if o >= 1:
                    wait_half_used(dve, o - 1, h)
                for j in range(ACT_HOT, HK):
                    k = HK * h + j
                    last = nc.vector.tensor_scalar(hot[0:HP, h, j, :], ids_bc[0:HP, o % 2, :],
                                                   row_id[0:HP, k:k + 1], None, ALU.is_equal)
                last.then_inc(hot_made_dve, 1)
                dve.wait_ge(tab_hi_made, c + 1)
                src = tab_raw[0:HP, o % 2, h * HK * D:(h + 1) * HK * D].rearrange("p (k d) -> p k d", d=D)
                nc.vector.tensor_tensor(tab_lo[0:HP, h, :, :], src, tab_hi[0:HP, h, :, :].bitcast(F32),
                                        ALU.subtract).then_inc(tab_lo_made, 1)

            half_table(0, 0)
            half_table(0, 1)
            for step in STEPS:
                kind = step[0]
                if kind in ("dense", "onehot", "batch"):
                    if kind == "onehot" and step[1] + 1 < NH:
                        half_table(step[1] + 1, 0)
                        half_table(step[1] + 1, 1)
                    i = FILL_OF[step]
                    if BY_DVE[i]:
                        dve.wait_ge(fill_made, i + 1)
                        fill_copy(nc.vector.tensor_copy, step, i % 2).then_inc(fill_copied_dve, 1)
                    if kind == "onehot" and step[1] == NH - 1:
                        dve.wait_ge(dense_w1_landed, 32)
                        nc.vector.tensor_tensor(w1_dense[:], w1_dense[:], w1_second[:], ALU.add) \
                            .then_inc(w1_summed, 1)
                elif kind == "gram":
                    _, t, u = step
                    i = PAIRS * t + u
                    dve.wait_ge(gram_made, i + 1)
                    if i == 0:
                        dve.wait_ge(ones_row_set, 1)
                    if i >= 2:
                        dve.wait_ge(prod_hi_made, i - 1)
                        dve.wait_ge(prod_lo_made, i - 1)
                    pack(nc.vector.tensor_copy, i, (2, 3)).then_inc(packed_dve, 1)
                    dve.wait_ge(prod_hi_made, i + 1)
                    if t >= 2:
                        dve.wait_ge(l1_made, t - 1)
                    cols = slice(PAIR_Q * u, PAIR_Q * (u + 1))
                    nc.vector.tensor_tensor(prod_lo[:, t % 2, :, cols], prod[:, i % 2, :, :],
                                            prod_hi[:, t % 2, :, cols].bitcast(F32), ALU.subtract) \
                        .then_inc(prod_lo_made, 1)
                elif kind == "l2":
                    t = step[1]
                    dve.wait_ge(l2_made, t + 1)
                    if t == 0:
                        dve.wait_ge(w3_landed, 16)
                    nc.vector.scalar_tensor_tensor(out=mlp_ps[:, 0:HID2], in0=mlp_ps[:, 0:HID2], scalar=0.0,
                                                   in1=w3_bc[:], op0=ALU.max, op1=ALU.mult,
                                                   accum_out=y[:, t:t + 1]).then_inc(y_made, 1)
                for k in W1_AFTER.get(step, ()):
                    dve.wait_ge(w1_hi_made, k + 1)
                    nc.vector.tensor_tensor(w1_lo[:, k, :], w1_raw[:, k, :], w1_hi[:, k, :].bitcast(F32),
                                            ALU.subtract).then_inc(w1_lo_made, 1)

        @block.tensor
        def _(pe):
            for step in STEPS:
                kind = step[0]
                if kind in ("dense", "onehot", "batch"):
                    i = FILL_OF[step]
                    if i >= 2:
                        wait_copied(pe, i - 2)
                    if kind == "onehot":
                        o = step[1]
                        for h in range(2):
                            c = 2 * o + h
                            pe.wait_ge(hot_made_dve, c + 1)
                            pe.wait_ge(hot_made_act, c + 1)
                            pe.wait_ge(tab_lo_made, c + 1)
                            for j in range(HK):
                                nc.tensor.matmul(fill_ps[:, i % 2, :], tab_hi[0:HP, h, j, :], hot[0:HP, h, j, :],
                                                 start=(h == 0 and j == 0), stop=False)
                                last = nc.tensor.matmul(fill_ps[:, i % 2, :], tab_lo[0:HP, h, j, :],
                                                        hot[0:HP, h, j, :], start=False,
                                                        stop=(h == 1 and j == HK - 1))
                            last.then_inc(first_half_used if h == 0 else fill_made, 1)
                        continue
                    if kind == "dense":
                        pe.wait_ge(ident_made, 1)
                        pe.wait_ge(dense_landed, 16)
                        vectors = [dense[:, t, :] for t in range(TILES)]
                    else:
                        n, size = step[1] * NB + step[2], len(BATCHES[step[2]])
                        pe.wait_ge(batch_landed[n % GSLOTS],
                                   16 * sum(len(BATCHES[k % NB]) for k in range(n % GSLOTS, n + 1, GSLOTS)))
                        vectors = [gathered[:, n % GSLOTS, j, :] for j in range(size)]
                    for j, v in enumerate(vectors):
                        last = nc.tensor.transpose(fill_ps[:, i % 2, j * P:(j + 1) * P], v, ident[:])
                    last.then_inc(fill_made, 1)
                elif kind == "gram":
                    _, t, u = step
                    i = PAIRS * t + u
                    if u == 0:
                        wait_copied(pe, LAST_FILL[t])
                    if i == 0:
                        pe.wait_ge(pads_zeroed, 1)
                    if i >= 2:
                        pe.wait_ge(packed_act, i - 1)
                        pe.wait_ge(packed_dve, i - 1)
                    for g in range(GROUPS):
                        q0 = PAIR_Q * u + S * g
                        b, gb = g // GPB, g % GPB
                        last = nc.tensor.matmul(gram_ps[:, i % 2, b, gb * S * COLS:(gb + 1) * S * COLS],
                                                vec[:, t, q0:q0 + S, :].rearrange("p q n -> p (q n)"),
                                                vec[:, t, q0:q0 + S, 0:COLS], start=True, stop=True)
                    last.then_inc(gram_made, 1)
                elif kind == "l1":
                    t = step[1]
                    pe.wait_ge(w1_summed, 1)
                    if t >= 1:
                        pe.wait_ge(y_made, t)
                    nc.tensor.matmul(mlp_ps[:], vec[:, t, :, 0], w1_dense[:], start=True, stop=False)
                    pe.wait_ge(w1_lo_made, KT)
                    pe.wait_ge(prod_lo_made, PAIRS * (t + 1))
                    for k in range(KT):
                        hi, lo = prod_hi[:, t % 2, k, :], prod_lo[:, t % 2, k, :]
                        nc.tensor.matmul(mlp_ps[:], hi, w1_hi[:, k, :], start=False, stop=False)
                        nc.tensor.matmul(mlp_ps[:], hi, w1_lo[:, k, :], start=False, stop=False)
                        last = nc.tensor.matmul(mlp_ps[:], lo, w1_hi[:, k, :], start=False, stop=(k == KT - 1))
                    last.then_inc(l1_made, 1)
                elif kind == "h1t":
                    t = step[1]
                    pe.wait_ge(h1_made, t + 1)
                    if t >= 1:
                        pe.wait_ge(h1t_copied, t)
                    for k in range(4):
                        last = nc.tensor.transpose(h1t_ps[:, k, :], h1[:, k * P:(k + 1) * P], ident[:])
                    last.then_inc(h1t_made, 1)
                elif kind == "l2":
                    t = step[1]
                    o = mlp_ps[:, 0:HID2]
                    pe.wait_ge(w2_landed, 32)
                    pe.wait_ge(ones_set, 1)
                    pe.wait_ge(h1_made, t + 1)
                    nc.tensor.matmul(o, ones[:], b2_sb[:], start=True, stop=False)
                    pe.wait_ge(h1t_copied, t + 1)
                    for k in range(4):
                        last = nc.tensor.matmul(o, h1t[:, k, :], w2_sb[:, k, :], start=False, stop=(k == 3))
                    last.then_inc(l2_made, 1)


def pair_rows(np, w1, b1):
    laid = np.zeros((KT, P, w1.shape[1]), w1.dtype)
    row = D
    for m in range(VECS):
        for n in range(m + 1, VECS):
            laid[m % KT, QUAD * (m // KT) + n] = w1[row]
            row += 1
    laid[0, ONE_ROW] = b1
    return laid


def kernel(**inputs):
    import numpy as np
    import concourse.bacc as bacc
    from concourse.bass_utils import run_bass_kernel_spmd as run

    nc = bacc.Bacc("TRN2", target_bir_lowering=False, num_devices=1)
    arrays, aps = {}, {}
    laid_out = {name: np.ascontiguousarray(a) for name, a in inputs.items()}
    laid_out["ids_t"] = np.ascontiguousarray(laid_out["ids"].T)
    laid_out["w1_pairs"] = pair_rows(np, laid_out["W_top1"], laid_out["b_top1"])
    for name, a in laid_out.items():
        arrays[f"in_{name}"] = a
        aps[name] = nc.dram_tensor(f"in_{name}", a.shape, mybir.dt.from_np(a.dtype), kind="ExternalInput").ap()
    out = nc.dram_tensor("out_y", (TILES * P, 1), F32, kind="ExternalOutput").ap()
    build(nc, aps, out)
    r = run(nc, [arrays], core_ids=[0])
    return r.results[0]["out_y"]
```

```python
from contextlib import ExitStack

import concourse.bass as bass
from concourse import mybir

F32 = mybir.dt.float32
F32R = mybir.dt.float32r
I32 = mybir.dt.int32
ALU = mybir.AluOpType
ACT = mybir.ActivationFunctionType

P = 128
TILES = 4
D = 128
FEATURES = 26
VECS = FEATURES + 1
NPAIRS = VECS * (VECS - 1) // 2
S = 4
QUAD = P // S
COLS = VECS
GPB = 4
PAIRS = 4
GROUPS = 2 * GPB
PAIR_Q = GROUPS * S
HID1, HID2 = 512, 256

BATCHES = [[0, 1, 4, 5], [9, 10, 11, 12], [13, 14, 15, 16], [17, 18, 19, 20], [22, 24]]
ONEHOT = [f for f in range(FEATURES) if not any(f in b for b in BATCHES)]
NB = len(BATCHES)
NH = len(ONEHOT)
TSLOTS = 3
GSLOTS = 8
ACT_HOT = (1, 0)

HP, HK = 125, 4

HALF = VECS // 2
KT = -(-(HALF + 1) // S)
WIDTHS = [[min(KT, HALF + 1 - KT * c), min(KT, HALF - KT * c)] for c in range(S)]
ONE_ROW = VECS


FEED_AT = [1, 0, 0, 0]
FIRST_FEED = 1


def order_of_work():
    out = [("dense",)]
    feeds = [("batch", t, i) for t in range(TILES) for i in range(NB)]
    for o in range(NH):
        out.append(("hot", o, 0))
        if o >= FIRST_FEED:
            out.append(feeds.pop(0))
        out.append(("hot", o, 1))
    for t in range(TILES):
        l1, h1t, l2 = [[("l1_dense", t - 1), ("l1", t - 1, 0)], [("h1t", t - 1, 0)],
                       [("l2_bias", t - 1), ("l2", t - 1, 0)]] if t else [[], [], []]
        work = [("gram", t, 0)] + l1 + [("gram", t, 1)] + h1t + [("gram", t, 2)]
        if t < TILES - 1:
            work += l2
        due = [f for f in feeds if f[1] <= t + 1]
        feeds = feeds[len(due):]
        for i in range(FEED_AT[t] - 1):
            out.append(due.pop(0))
        if FEED_AT[t] and due:
            out.append(due.pop(0))
        while work or due:
            if work:
                out.append(work.pop(0))
            if due and out[-1][0] not in ("l1_dense", "l2_bias"):
                out.append(due.pop(0))
        out.append(("gram", t, PAIRS - 1))
    t = TILES - 1
    out += [("l1_dense", t), *l2, ("l1", t, 0), ("l1", t, 1), ("h1t", t, 0), ("l2_bias", t), ("h1t", t, 1),
            ("l2", t, 0), ("l2", t, 1)]
    return out


STEPS = order_of_work()
SERVED, to_split = [], None
for n, s in enumerate(STEPS):
    SERVED.append(s)
    last = s if s[0] == "gram" else STEPS[n - 1] if s[0] == "batch" else None
    if last is not None and last[0] == "gram" and STEPS[n + 1][0] != "batch":
        if to_split:
            SERVED.append(("split", *to_split))
        SERVED.append(("merge", *last[1:]))
        to_split = last[1:]
        if to_split[1] == PAIRS - 1:
            SERVED.append(("split", *to_split))
            to_split = None
FILLS = [s for s in STEPS if s[0] in ("dense", "batch") or (s[0] == "hot" and s[2] == 1)]
FILL_OF = {s: i for i, s in enumerate(FILLS)}
LAST_FILL = [max(i for i, s in enumerate(FILLS) if s[0] != "batch" or s[1] == t) for t in range(TILES)]
LAST_HOT = FILL_OF[("hot", NH - 1, 1)]


def banks():
    bank, before, held, current, inside = {}, {}, [None, None], 1, False
    for step in STEPS:
        if step[0] == "hot" and step[2] == 1:
            inside = False
        elif step[0] in ("dense", "batch", "hot"):
            i = FILL_OF[("hot", step[1], 1) if step[0] == "hot" else step]
            if not inside:
                current = 1 - current
            bank[i] = 1 - current if inside else current
            before[i] = held[bank[i]]
            held[bank[i]] = i
            inside = step[0] == "hot"
    return bank, before


def parts(t):
    return 2 if t == TILES - 1 else 1


BANK, BEFORE = banks()
BY_DVE = [False] * len(FILLS)

W1_HI_STEPS = [("hot", o, 1) for o in range(3, NH)] + [("gram", 0, u) for u in range(PAIRS)]
W1_LO_STEPS = [("hot", NH - 1, 1)] + [("gram", 0, u) for u in range(PAIRS)]


def spread(steps):
    return {step: [k for k in range(KT) if k * len(steps) // KT == i] for i, step in enumerate(steps)}


W1_HI_AFTER, W1_LO_AFTER = spread(W1_HI_STEPS), spread(W1_LO_STEPS)
W1_LOADS = {o: [k for k in range(KT) if k * (NH - 3) // KT == o - 3] for o in range(3, NH)}


def build(nc, ins, out):
    tables = [ins[f"tbl_{f}"] for f in range(FEATURES)]
    W1, W2 = ins["W_top1"], ins["W_top2"]
    assert all(tables[f].shape[0] == HP * 2 * HK for f in ONEHOT)

    with ExitStack() as ctx:
        def sb(name, shape, dt):
            return ctx.enter_context(nc.sbuf_tensor(name, shape, dt))

        def sem(name):
            return ctx.enter_context(nc.semaphore(name))

        vec = sb("vec", [P, TILES, P, QUAD], F32)
        gathered = sb("gathered", [P, GSLOTS, 4, D], F32)
        dense = sb("dense", [P, TILES, D], F32)
        ids_sb = sb("ids_sb", [P, TILES, FEATURES], I32)
        ident = sb("ident", [P, P], F32)
        row_id_i = sb("row_id_i", [P, 2 * HK], I32)
        row_id = sb("row_id", [P, 2 * HK], F32)
        minus_row_id = sb("minus_row_id", [P, 2 * HK], F32)
        one_col = sb("one_col", [P, 1], F32)
        tab_raw = sb("tab_raw", [P, TSLOTS, 2 * HK * D], F32)
        ids_bc = sb("ids_bc", [P, TSLOTS, TILES * P], I32)
        tab_hi = sb("tab_hi", [P, 2, HK, D], F32R)
        tab_lo = sb("tab_lo", [P, 2, HK, D], F32R)
        hot = sb("hot", [P, 2, HK, TILES * P], F32R)
        w1_raw = sb("w1_raw", [P, KT, HID1], F32)
        w1_hi = sb("w1_hi", [P, KT, HID1], F32R)
        w1_lo = sb("w1_lo", [P, KT, HID1], F32R)
        w1_dense = sb("w1_dense", [P, HID1], F32)
        w1_second = sb("w1_second", [P, HID1], F32)
        w2_sb = sb("w2_sb", [P, 4, HID2], F32)
        b2_sb = sb("b2_sb", [1, HID2], F32)
        ones = sb("ones", [1, P], F32)
        ones_r = sb("ones_r", [1, P], F32R)
        b2_hi = sb("b2_hi", [1, HID2], F32R)
        b2_lo = sb("b2_lo", [1, HID2], F32R)
        w3_bc = sb("w3_bc", [P, HID2], F32)
        prod = sb("prod", [P, 2, 2, KT, PAIR_Q], F32)
        shares = sb("shares", [P, 2, KT], F32)
        prod_hi = sb("prod_hi", [P, 2, KT, P], F32R)
        prod_lo = sb("prod_lo", [P, 2, KT, P], F32R)
        h1 = sb("h1", [P, HID1], F32)
        h1t = sb("h1t", [P, 4, P], F32)
        y = sb("y", [P, TILES], F32)

        fill_ps = ctx.enter_context(nc.psum_tensor("fill_ps", [P, 2, 512], F32))
        gram_ps = ctx.enter_context(nc.psum_tensor("gram_ps", [P, 2, 2, 512], F32))
        mlp_ps = ctx.enter_context(nc.psum_tensor("mlp_ps", [P, 512], F32))
        h1t_ps = ctx.enter_context(nc.psum_tensor("h1t_ps", [P, 4, P], F32))

        ids_landed = sem("ids_landed")
        dense_landed = sem("dense_landed")
        w1_landed = [sem(f"w1_landed{k}") for k in range(KT)]
        dense_w1_landed = sem("dense_w1_landed")
        w2_landed = sem("w2_landed")
        w3_landed = sem("w3_landed")
        b2_landed = sem("b2_landed")
        b2_split = sem("b2_split")
        table_landed = [sem(f"table_landed{i}") for i in range(TSLOTS)]
        bc_landed = [sem(f"bc_landed{i}") for i in range(TSLOTS)]
        batch_landed = [sem(f"batch_landed{i}") for i in range(GSLOTS)]
        ident_zeroed = sem("ident_zeroed")
        ident_made = sem("ident_made")
        row_ids_made = sem("row_ids_made")
        row_ids_cast = sem("row_ids_cast")
        pads_zeroed = sem("pads_zeroed")
        prod_zeroed = sem("prod_zeroed")
        ones_row_set = sem("ones_row_set")
        ones_set = sem("ones_set")
        tab_hi_made = sem("tab_hi_made")
        tab_lo_made = sem("tab_lo_made")
        distance_made = sem("distance_made")
        hot_made_act = sem("hot_made_act")
        hot_made_dve = sem("hot_made_dve")
        hot_used = sem("hot_used")
        fill_made = sem("fill_made")
        fill_copied_act = sem("fill_copied_act")
        fill_copied_dve = sem("fill_copied_dve")
        gram_made = sem("gram_made")
        packed_act = sem("packed_act")
        packed_dve = sem("packed_dve")
        shares_landed = sem("shares_landed")
        shared = sem("shared")
        merged = sem("merged")
        prod_hi_made = sem("prod_hi_made")
        prod_lo_made = sem("prod_lo_made")
        w1_summed = sem("w1_summed")
        w1_hi_made = sem("w1_hi_made")
        w1_lo_made = sem("w1_lo_made")
        l1_made = sem("l1_made")
        h1_made = sem("h1_made")
        h1t_made = sem("h1t_made")
        h1t_copied = sem("h1t_copied")
        l2_made = sem("l2_made")
        y_made = sem("y_made")
        out_written = sem("out_written")

        def fill_copy(copy, step, bank):
            src = fill_ps[:, bank, :]
            if step[0] == "hot":
                return copy(vec[:, :, :, ONEHOT[step[1]] + 1], src.rearrange("p (q t) -> p t q", t=TILES))
            if step[0] == "dense":
                return copy(vec[:, :, :, 0], src.rearrange("p (t q) -> p t q", t=TILES))
            fs = BATCHES[step[2]]
            n, first, by = len(fs), fs[0] + 1, fs[1] - fs[0]
            slots = vec[:, step[1], :, :]
            if all(b - a == by for a, b in zip(fs, fs[1:])):
                return copy(slots[:, :, first:fs[-1] + 2:by].rearrange("p q n -> p n q"),
                            src[:, 0:n * P].rearrange("p (n q) -> p n q", n=n))
            gap = fs[2] - fs[0]
            assert by == 1 and fs == [fs[0], fs[0] + 1, fs[0] + gap, fs[0] + gap + 1]
            return copy(slots[:, :, first:first + 2 * gap].rearrange("p q (a n) -> p a n q", a=2)[:, :, 0:2, :],
                        src.rearrange("p (a n q) -> p a n q", a=2, n=2))

        def wait_copied(eng, i):
            n = sum(BY_DVE[:i + 1])
            eng.wait_ge(fill_copied_act, i + 1 - n)
            if n:
                eng.wait_ge(fill_copied_dve, n)

        def l1_part(t, p):
            if parts(t) == 1:
                return mlp_ps[:], slice(0, HID1)
            n = HID1 // parts(t)
            return fill_ps[:, p, 0:n], slice(p * n, (p + 1) * n)

        def h1t_part(t, p):
            n = 4 // parts(t)
            bank = h1t_ps if p == 0 else gram_ps[:, 0, 0, :].rearrange("p (k q) -> p k q", k=4)
            return bank[:, 0:n, :], slice(n * p, n * (p + 1))

        def act_hots(o, h):
            return sum(ACT_HOT) * o + sum(ACT_HOT[:h + 1])

        def dve_hots(o, h):
            return HK * (2 * o + h + 1) - act_hots(o, h)

        def hot_order(h):
            return list(range(ACT_HOT[h], HK)) + list(range(ACT_HOT[h]))

        def wait_used(eng, o, h, n):
            if (h, n) == (1, HK - 1):
                eng.wait_ge(fill_made, FILL_OF[("hot", o, 1)] + 1)
            else:
                eng.wait_ge(hot_used, o * (2 * HK - 1) + HK * h + n + 1)

        def pack(copy, i, quadrants):
            for s in quadrants:
                own = gram_ps[QUAD * s:QUAD * s + VECS, i % 2, :, 0:GPB * S * COLS] \
                    .rearrange("p b (g a) -> p b g a", g=GPB)
                for c in range(S):
                    for kind, m in enumerate((KT * c + HALF, KT * c)):
                        to = prod[QUAD * c:QUAD * c + VECS, i % 2, kind, 0:WIDTHS[c][kind], :]
                        last = copy(to.rearrange("p j (b g s) -> p b g j s", b=2, s=S)[:, :, :, :, s],
                                    own[:, :, :, s * COLS + m:s * COLS + m + WIDTHS[c][kind]])
            return last

        block = ctx.enter_context(nc.Block())

        @block.sync
        def _(sp):
            def load_table(o):
                f = ONEHOT[o]
                if o >= TSLOTS:
                    sp.wait_ge(hot_made_dve, dve_hots(o - TSLOTS, 1))
                    sp.wait_ge(hot_made_act, act_hots(o - TSLOTS, 1))
                sp.dma_start(ids_bc[:, o % TSLOTS, :], ins["ids_t"][f:f + 1, :].to_broadcast([P, TILES * P])) \
                    .then_inc(bc_landed[o % TSLOTS], 16)
                if o >= TSLOTS:
                    sp.wait_ge(tab_lo_made, 2 * (o - TSLOTS + 1))
                src = tables[f].rearrange("(p k) d -> p (k d)", p=HP)
                for a, b in ((0, 112), (112, HP)):
                    sp.dma_start(tab_raw[a:b, o % TSLOTS, :], src[a:b, :]).then_inc(table_landed[o % TSLOTS], 16)

            sp.dma_start(ids_sb[:], ins["ids"].rearrange("(q t) f -> q t f", t=TILES)).then_inc(ids_landed, 16)
            load_table(0)
            sp.dma_start(shares[:], ins["shares"]).then_inc(shares_landed, 16)
            sp.dma_start(dense[:], ins["r_dense_proj"].rearrange("(q t) d -> q t d", t=TILES)) \
                .then_inc(dense_landed, 16)
            load_table(1)
            load_table(2)
            sp.dma_start(w1_dense[:], W1[0:D, :]).then_inc(dense_w1_landed, 16)
            sp.dma_start(w1_second[:], W1[D + NPAIRS:D + NPAIRS + D, :]).then_inc(dense_w1_landed, 16)
            for o in range(3, NH):
                load_table(o)
                for k in W1_LOADS[o]:
                    sp.dma_start(w1_raw[:, k, :], ins["w1_pairs"][k]).then_inc(w1_landed[k], 16)
            sp.dma_start(w2_sb[:], W2.rearrange("(k p) n -> p k n", p=P)).then_inc(w2_landed, 16)
            sp.dma_start(b2_sb[:], ins["b_top2"].rearrange("(a n) -> a n", a=1)).then_inc(b2_landed, 16)
            sp.dma_start(w3_bc[:], ins["W_top3"].rearrange("n o -> o n").to_broadcast([P, HID2])) \
                .then_inc(w3_landed, 16)
            sp.wait_ge(y_made, TILES)
            sp.dma_start(out.rearrange("(q t) o -> q (t o)", t=TILES), y[:]).then_inc(out_written, 16)
            sp.wait_ge(out_written, 16)

        @block.gpsimd
        def _(pool):
            nc.gpsimd.memset(ident[:], 0.0).then_inc(ident_zeroed, 1)
            nc.gpsimd.iota(row_id_i[:], pattern=[[1, 2 * HK]], base=0, channel_multiplier=2 * HK) \
                .then_inc(row_ids_made, 1)
            pool.wait_ge(ident_zeroed, 1)
            nc.gpsimd.affine_select(out=ident[:], in_=ident[:], compare_op=ALU.not_equal, fill=1.0, base=0,
                                    pattern=[[-1, P]], channel_multiplier=1).then_inc(ident_made, 1)
            nc.gpsimd.memset(prod[:], 0.0).then_inc(prod_zeroed, 1)
            pool.wait_ge(ids_landed, 16)
            for t in range(TILES):
                for i in range(NB):
                    n = t * NB + i
                    if n >= GSLOTS:
                        old = n - GSLOTS
                        pool.wait_ge(fill_made, FILL_OF[("batch", old // NB, old % NB)] + 1)
                    for j, f in enumerate(BATCHES[i]):
                        pool.indirect_dma_start(
                            out=gathered[:, n % GSLOTS, j, :], out_offset=None, in_=tables[f],
                            in_offset=bass.IndirectOffsetOnAxis(ap=ids_sb[:, t, f:f + 1], axis=0),
                        ).then_inc(batch_landed[n % GSLOTS], 16)

        @block.scalar
        def _(act):
            def half_table(o, h):
                c = 2 * o + h
                act.wait_ge(row_ids_cast, 2)
                act.wait_ge(bc_landed[o % TSLOTS], 16 * (o // TSLOTS + 1))
                act.wait_ge(table_landed[o % TSLOTS], 32 * (o // TSLOTS + 1))
                src = tab_raw[0:HP, o % TSLOTS, h * HK * D:(h + 1) * HK * D].rearrange("p (k d) -> p k d", d=D)
                if o >= 1:
                    wait_used(act, o - 1, h, 0)
                nc.scalar.copy(tab_hi[0:HP, h, :, :], src).then_inc(tab_hi_made, 1)
                if o >= 1 and ACT_HOT[h]:
                    wait_used(act, o - 1, h, HK - 1)
                for j in range(ACT_HOT[h]):
                    k = HK * h + j
                    nc.scalar.activation(hot[0:HP, h, j, :], ids_bc[0:HP, o % TSLOTS, :], ACT.Abs,
                                         bias=minus_row_id[0:HP, k:k + 1]).then_inc(distance_made, 1)
                if ACT_HOT[h]:
                    act.wait_ge(distance_made, act_hots(o, h))
                    act.wait_ge(ones_set, 2)
                for j in range(ACT_HOT[h]):
                    nc.scalar.activation(hot[0:HP, h, j, :], hot[0:HP, h, j, :].bitcast(F32), ACT.Relu,
                                         bias=one_col[0:HP, :], scale=-1.0).then_inc(hot_made_act, 1)

            half_table(0, 0)
            half_table(0, 1)
            for step in SERVED:
                kind = step[0]
                if step in FILL_OF and not BY_DVE[FILL_OF[step]]:
                    i = FILL_OF[step]
                    act.wait_ge(fill_made, i + 1)
                    act.wait_ge(pads_zeroed, 1)
                    fill_copy(nc.scalar.copy, step, BANK[i]).then_inc(fill_copied_act, 1)
                if kind == "hot" and step[1] + 1 < NH:
                    half_table(step[1] + 1, step[2])
                if kind == "gram":
                    _, t, u = step
                    i = PAIRS * t + u
                    act.wait_ge(gram_made, i + 1)
                    if i == 0:
                        act.wait_ge(ones_row_set, 1)
                    if i >= 2:
                        act.wait_ge(prod_lo_made, i - 1)
                        act.wait_ge(prod_hi_made, i - 1)
                    pack(nc.scalar.copy, i, (0, 1)).then_inc(packed_act, 1)
                elif kind == "split":
                    _, t, u = step
                    i = PAIRS * t + u
                    act.wait_ge(merged, i + 1)
                    if t >= 2:
                        act.wait_ge(l1_made, t - 1)
                    nc.scalar.copy(prod_hi[:, t % 2, :, PAIR_Q * u:PAIR_Q * (u + 1)], prod[:, i % 2, 0, :, :]) \
                        .then_inc(prod_hi_made, 1)
                elif kind == "l1":
                    _, t, p = step
                    act.wait_ge(l1_made, t + p + 1)
                    if t >= 1 and p == 0:
                        act.wait_ge(h1t_made, t)
                    bank, cols = l1_part(t, p)
                    nc.scalar.activation(h1[:, cols], bank, ACT.Relu).then_inc(h1_made, 1)
                elif kind == "h1t":
                    _, t, p = step
                    act.wait_ge(h1t_made, t + p + 1)
                    if t >= 1 and p == 0:
                        act.wait_ge(l2_made, t)
                    bank, ks = h1t_part(t, p)
                    nc.scalar.copy(h1t[:, ks, :], bank).then_inc(h1t_copied, 1)
                for k in W1_HI_AFTER.get(step, ()):
                    act.wait_ge(w1_landed[k], 16)
                    nc.scalar.copy(w1_hi[:, k, :], w1_raw[:, k, :]).then_inc(w1_hi_made, 1)

        @block.vector
        def _(dve):
            nc.vector.memset(ones[:], 1.0).then_inc(ones_set, 1)
            nc.vector.memset(one_col[:], 1.0).then_inc(ones_set, 1)
            dve.wait_ge(row_ids_made, 1)
            nc.vector.tensor_copy(row_id[:], row_id_i[:]).then_inc(row_ids_cast, 1)
            nc.vector.tensor_scalar(minus_row_id[:], row_id_i[:], -1.0, None, ALU.mult).then_inc(row_ids_cast, 1)
            nc.vector.memset(vec[:, :, :, VECS:QUAD], 0.0).then_inc(pads_zeroed, 1)
            dve.wait_ge(prod_zeroed, 1)
            nc.vector.memset(prod[0:QUAD, :, 0, 0, :], 1.0).then_inc(ones_row_set, 1)
            dve.wait_ge(row_ids_cast, 2)

            def half_table(o, h):
                c = 2 * o + h
                dve.wait_ge(bc_landed[o % TSLOTS], 16 * (o // TSLOTS + 1))
                for n, j in enumerate(range(ACT_HOT[h], HK)):
                    k = HK * h + j
                    if o >= 1:
                        wait_used(dve, o - 1, h, n)
                    nc.vector.tensor_scalar(hot[0:HP, h, j, :], ids_bc[0:HP, o % TSLOTS, :],
                                            row_id[0:HP, k:k + 1], None, ALU.is_equal).then_inc(hot_made_dve, 1)
                dve.wait_ge(tab_hi_made, c + 1)
                src = tab_raw[0:HP, o % TSLOTS, h * HK * D:(h + 1) * HK * D].rearrange("p (k d) -> p k d", d=D)
                if o >= 1:
                    wait_used(dve, o - 1, h, HK - 1)
                nc.vector.tensor_tensor(tab_lo[0:HP, h, :, :], src, tab_hi[0:HP, h, :, :].bitcast(F32),
                                        ALU.subtract).then_inc(tab_lo_made, 1)

            half_table(0, 0)
            half_table(0, 1)
            for step in SERVED:
                kind = step[0]
                if step in FILL_OF and BY_DVE[FILL_OF[step]]:
                    i = FILL_OF[step]
                    dve.wait_ge(fill_made, i + 1)
                    fill_copy(nc.vector.tensor_copy, step, BANK[i]).then_inc(fill_copied_dve, 1)
                if kind == "hot":
                    if step[1] + 1 < NH:
                        half_table(step[1] + 1, step[2])
                    elif step[2] == 1:
                        dve.wait_ge(dense_w1_landed, 32)
                        nc.vector.tensor_tensor(w1_dense[:], w1_dense[:], w1_second[:], ALU.add) \
                            .then_inc(w1_summed, 1)
                        dve.wait_ge(ones_set, 2)
                        dve.wait_ge(b2_landed, 16)
                        nc.vector.tensor_copy(ones_r[:], ones[:]).then_inc(b2_split, 1)
                        nc.vector.tensor_copy(b2_hi[:], b2_sb[:]).then_inc(b2_split, 1)
                        dve.wait_ge(b2_split, 2)
                        nc.vector.tensor_tensor(b2_lo[:], b2_sb[:], b2_hi[:].bitcast(F32), ALU.subtract) \
                            .then_inc(b2_split, 1)
                elif kind == "gram":
                    _, t, u = step
                    i = PAIRS * t + u
                    dve.wait_ge(gram_made, i + 1)
                    if i == 0:
                        dve.wait_ge(ones_row_set, 1)
                    if i >= 2:
                        dve.wait_ge(prod_hi_made, i - 1)
                        dve.wait_ge(prod_lo_made, i - 1)
                    pack(nc.vector.tensor_copy, i, (2, 3)).then_inc(packed_dve, 1)
                elif kind == "merge":
                    _, t, u = step
                    i = PAIRS * t + u
                    dve.wait_ge(packed_act, i + 1)
                    dve.wait_ge(packed_dve, i + 1)
                    if i == 0:
                        dve.wait_ge(shares_landed, 16)
                    both = prod[:, i % 2, :, :, :]
                    nc.vector.tensor_tensor(both, both, shares[:].unsqueeze(3).to_broadcast([P, 2, KT, PAIR_Q]),
                                            ALU.mult).then_inc(shared, 1)
                    dve.wait_ge(shared, i + 1)
                    nc.vector.tensor_tensor(both[:, 0], both[:, 0], both[:, 1], ALU.add).then_inc(merged, 1)
                elif kind == "split":
                    _, t, u = step
                    i = PAIRS * t + u
                    dve.wait_ge(prod_hi_made, i + 1)
                    if t >= 2:
                        dve.wait_ge(l1_made, t - 1)
                    cols = slice(PAIR_Q * u, PAIR_Q * (u + 1))
                    nc.vector.tensor_tensor(prod_lo[:, t % 2, :, cols], prod[:, i % 2, 0, :, :],
                                            prod_hi[:, t % 2, :, cols].bitcast(F32), ALU.subtract) \
                        .then_inc(prod_lo_made, 1)
                elif kind == "l2" and step[2] == parts(step[1]) - 1:
                    t = step[1]
                    dve.wait_ge(l2_made, t + 1)
                    if t == 0:
                        dve.wait_ge(w3_landed, 16)
                    nc.vector.scalar_tensor_tensor(out=mlp_ps[:, 0:HID2], in0=mlp_ps[:, 0:HID2], scalar=0.0,
                                                   in1=w3_bc[:], op0=ALU.max, op1=ALU.mult,
                                                   accum_out=y[:, t:t + 1]).then_inc(y_made, 1)
                for k in W1_LO_AFTER.get(step, ()):
                    dve.wait_ge(w1_hi_made, k + 1)
                    nc.vector.tensor_tensor(w1_lo[:, k, :], w1_raw[:, k, :], w1_hi[:, k, :].bitcast(F32),
                                            ALU.subtract).then_inc(w1_lo_made, 1)

        @block.tensor
        def _(pe):
            for step in STEPS:
                kind = step[0]
                if kind in ("dense", "hot", "batch"):
                    i = FILL_OF[("hot", step[1], 1) if kind == "hot" else step]
                    if BEFORE[i] is not None and not (kind == "hot" and step[2] == 1):
                        wait_copied(pe, BEFORE[i])
                    into = fill_ps[:, BANK[i], :]
                    if kind == "hot":
                        _, o, h = step
                        c = 2 * o + h
                        pe.wait_ge(tab_hi_made, c + 1)
                        for n, j in enumerate(hot_order(h)):
                            if j < ACT_HOT[h]:
                                pe.wait_ge(hot_made_act, act_hots(o, h) - (ACT_HOT[h] - 1 - j))
                            else:
                                pe.wait_ge(hot_made_dve, dve_hots(o, h) - (HK - 1 - j))
                            nc.tensor.matmul(into, tab_hi[0:HP, h, j, :], hot[0:HP, h, j, :],
                                             start=(h == 0 and n == 0), stop=False)
                        pe.wait_ge(tab_lo_made, c + 1)
                        for n, j in enumerate(hot_order(h)):
                            used = nc.tensor.matmul(into, tab_lo[0:HP, h, j, :], hot[0:HP, h, j, :],
                                                    start=False, stop=(h == 1 and n == HK - 1))
                            used.then_inc(fill_made if (h, n) == (1, HK - 1) else hot_used, 1)
                        continue
                    if kind == "dense":
                        pe.wait_ge(ident_made, 1)
                        pe.wait_ge(dense_landed, 16)
                        vectors = [dense[:, t, :] for t in range(TILES)]
                    else:
                        n, size = step[1] * NB + step[2], len(BATCHES[step[2]])
                        pe.wait_ge(batch_landed[n % GSLOTS],
                                   16 * sum(len(BATCHES[k % NB]) for k in range(n % GSLOTS, n + 1, GSLOTS)))
                        vectors = [gathered[:, n % GSLOTS, j, :] for j in range(size)]
                    for j, v in enumerate(vectors):
                        last = nc.tensor.transpose(into[:, j * P:(j + 1) * P], v, ident[:])
                    last.then_inc(fill_made, 1)
                elif kind == "gram":
                    _, t, u = step
                    i = PAIRS * t + u
                    if u == 0:
                        wait_copied(pe, LAST_FILL[t])
                    if i == 0:
                        pe.wait_ge(pads_zeroed, 1)
                    if i >= 2:
                        pe.wait_ge(packed_act, i - 1)
                        pe.wait_ge(packed_dve, i - 1)
                    for g in range(GROUPS):
                        q0 = PAIR_Q * u + S * g
                        b, gb = g // GPB, g % GPB
                        last = nc.tensor.matmul(gram_ps[:, i % 2, b, gb * S * COLS:(gb + 1) * S * COLS],
                                                vec[:, t, q0:q0 + S, :].rearrange("p q n -> p (q n)"),
                                                vec[:, t, q0:q0 + S, 0:COLS], start=True, stop=True)
                    last.then_inc(gram_made, 1)
                elif kind == "l1_dense":
                    t = step[1]
                    pe.wait_ge(w1_summed, 1)
                    if parts(t) == 1 and t >= 1:
                        pe.wait_ge(y_made, t)
                    for p in range(parts(t)):
                        if parts(t) > 1:
                            wait_copied(pe, max(i for i in BANK if BANK[i] == p))
                        bank, cols = l1_part(t, p)
                        nc.tensor.matmul(bank, vec[:, t, :, 0], w1_dense[:, cols], start=True, stop=False)
                elif kind == "l1":
                    _, t, p = step
                    bank, cols = l1_part(t, p)
                    pe.wait_ge(w1_hi_made, KT)
                    pe.wait_ge(w1_lo_made, KT)
                    pe.wait_ge(prod_hi_made, PAIRS * (t + 1))
                    for k in range(KT):
                        hi = prod_hi[:, t % 2, k, :]
                        nc.tensor.matmul(bank, hi, w1_hi[:, k, cols], start=False, stop=False)
                        nc.tensor.matmul(bank, hi, w1_lo[:, k, cols], start=False, stop=False)
                    pe.wait_ge(prod_lo_made, PAIRS * (t + 1))
                    for k in range(KT):
                        last = nc.tensor.matmul(bank, prod_lo[:, t % 2, k, :], w1_hi[:, k, cols],
                                                start=False, stop=(k == KT - 1))
                    last.then_inc(l1_made, 1)
                elif kind == "h1t":
                    _, t, p = step
                    pe.wait_ge(h1_made, t + p + 1)
                    if t >= 1 and p == 0:
                        pe.wait_ge(h1t_copied, t)
                    bank, ks = h1t_part(t, p)
                    if p > 0:
                        pe.wait_ge(packed_act, PAIRS * TILES)
                        pe.wait_ge(packed_dve, PAIRS * TILES)
                    for n, k in enumerate(range(ks.start, ks.stop)):
                        last = nc.tensor.transpose(bank[:, n, :], h1[:, k * P:(k + 1) * P], ident[:])
                    last.then_inc(h1t_made, 1)
                elif kind == "l2_bias":
                    t = step[1]
                    pe.wait_ge(b2_split, 3)
                    if parts(t) == 1:
                        pe.wait_ge(h1_made, t + 1)
                    else:
                        pe.wait_ge(y_made, t)
                    nc.tensor.matmul(mlp_ps[:, 0:HID2], ones_r[:], b2_hi[:], start=True, stop=False)
                    nc.tensor.matmul(mlp_ps[:, 0:HID2], ones_r[:], b2_lo[:], start=False, stop=False)
                elif kind == "l2":
                    _, t, p = step
                    pe.wait_ge(w2_landed, 16)
                    pe.wait_ge(h1t_copied, t + p + 1)
                    for k in range(4 // parts(t) * p, 4 // parts(t) * (p + 1)):
                        last = nc.tensor.matmul(mlp_ps[:, 0:HID2], h1t[:, k, :], w2_sb[:, k, :],
                                                start=False, stop=(k == 3))
                    if p == parts(t) - 1:
                        last.then_inc(l2_made, 1)


def owner(slot, n):
    return slot if slot < HALF and slot < n <= slot + HALF else slot + HALF


def slots_of_rows():
    return [(slot % KT, slot // KT, slot, n) for slot in range(HALF + 1) for n in range(VECS)]


def kinds_of_rows(np):
    kinds = np.zeros((P, 2, KT), np.float32)
    kinds[:, 0] = 1
    for j, c, slot, n in slots_of_rows():
        if owner(slot, n) == slot:
            kinds[QUAD * c + n, :, j] = 0, 1
    return kinds


def pair_rows(np, w1, b1):
    laid = np.zeros((KT, P, w1.shape[1]), w1.dtype)
    row_of = {}
    for m in range(VECS):
        for n in range(m + 1, VECS):
            row_of[m, n] = D + len(row_of)
    for j, c, slot, n in slots_of_rows():
        m = owner(slot, n)
        if 1 <= (n - m) % VECS <= HALF:
            laid[j, QUAD * c + n] = w1[row_of.pop((min(m, n), max(m, n)))]
    assert not row_of
    laid[0, ONE_ROW] = b1
    return laid


def kernel(**inputs):
    import numpy as np
    import concourse.bacc as bacc
    from concourse.bass_utils import run_bass_kernel_spmd as run

    nc = bacc.Bacc("TRN2", target_bir_lowering=False, num_devices=1)
    arrays, aps = {}, {}
    laid_out = {name: np.ascontiguousarray(a) for name, a in inputs.items()}
    laid_out["ids_t"] = np.ascontiguousarray(laid_out["ids"].T)
    laid_out["w1_pairs"] = pair_rows(np, laid_out["W_top1"], laid_out["b_top1"])
    laid_out["shares"] = kinds_of_rows(np)
    for name, a in laid_out.items():
        arrays[f"in_{name}"] = a
        aps[name] = nc.dram_tensor(f"in_{name}", a.shape, mybir.dt.from_np(a.dtype), kind="ExternalInput").ap()
    out = nc.dram_tensor("out_y", (TILES * P, 1), F32, kind="ExternalOutput").ap()
    build(nc, aps, out)
    r = run(nc, [arrays], core_ids=[0])
    return r.results[0]["out_y"]
```
